# Optimizing a Trainium2 kernel written in Bass

```python
import numpy as np
import jax
import jax.numpy as jnp

def _softmax(x, axis=-1):
    return jax.nn.softmax(x, axis=axis)

def _gelu(x):
    return jax.nn.gelu(x, approximate=True)

def _silu(x):
    return jax.nn.silu(x)

def _sigmoid(x):
    return jax.nn.sigmoid(x)

def _layernorm(x, axis=-1, eps=1e-05):
    m = jnp.mean(x, axis=axis, keepdims=True)
    v = jnp.var(x, axis=axis, keepdims=True)
    return (x - m) / jnp.sqrt(v + eps)

def _scatter_add(tgt, idx, src, axis=0):
    return tgt.at[idx].add(src)

def _segment_sum(src, seg, n):
    return jax.ops.segment_sum(src, seg, n)
kernel_name = 'mk_flamingo_gated_d1_seqx_r4_d9c9ec'

def setup_inputs(seed: int=0):
    np.random.seed(seed)
    _w = jnp.asarray

    def _rec_inputs():
        import jax
        import jax.numpy as jnp
        _rk = jax.random.key(seed)
        x = 7.22e-05 + 1 * jax.random.normal(jax.random.fold_in(_rk, 1), (4, 512, 512), jnp.float32)
        _lenS = 512 - jax.random.randint(jax.random.fold_in(_rk, 7), (4,), 0, max(1, 512 // 4) + 1, jnp.int32)
        _lenS2 = 512 - jax.random.randint(jax.random.fold_in(_rk, 8), (4,), 0, max(1, 512 // 4) + 1, jnp.int32)
        _ctx_1024P = jax.random.normal(jax.random.fold_in(_rk, 11), (4, 16, 256), jnp.float32)
        _ctx_1024c = jax.random.dirichlet(jax.random.fold_in(_rk, 511), 0.3 * jnp.ones((16,), jnp.float32), (4, 512))
        _ctx_1024t = jnp.einsum('bsk,bkd->bsd', _ctx_1024c, _ctx_1024P)
        _ctx_1024t = _ctx_1024t * jax.lax.rsqrt(jnp.mean(jnp.square(_ctx_1024t)) + 1e-12) * 0.953939
        ctx_1024 = 2.81802e-05 + 1.00001 * (_ctx_1024t + 0.3 * jax.random.normal(jax.random.fold_in(_rk, 611), (4, 512, 256), jnp.float32))
        _g = jax.random.normal(jax.random.fold_in(_rk, 9001), (2, 1), jnp.float32)
        _g = jnp.sign(_g) * jnp.maximum(jnp.abs(_g), 1.0) + (_g == 0) * 1.0
        g_xattn = _g[0]
        g_ffn = _g[1]
        return (x, ctx_1024, g_xattn, g_ffn)
    x, ctx_1024, g_xattn, g_ffn = _rec_inputs()

    def _L0_xattn_setup():
        import jax, jax.numpy as jnp
        import numpy as np
        key = jax.random.key(seed)
        ks = jax.random.split(key, 6)
        B, L, N, C, D = (8, 128, 512, 256, 128)
        return {'teacher_logits': jax.random.normal(ks[0], (B, L, N), dtype=jnp.float32), 'teacher_features': jax.random.normal(ks[1], (B, N, C), dtype=jnp.float32), 'Wq': jax.random.normal(ks[2], (D, C), dtype=jnp.float32) * (1.0 / np.sqrt(C)), 'bq': jnp.zeros((D,), dtype=jnp.float32), 'Wk': jax.random.normal(ks[3], (D, C), dtype=jnp.float32) * (1.0 / np.sqrt(C)), 'bk': jnp.zeros((D,), dtype=jnp.float32)}
    _L0_xattn_all = _L0_xattn_setup()
    _L0_xattn_in = {k: v for k, v in _L0_xattn_all.items() if k in ('Wq', 'bq', 'Wk', 'bk')}
    del _L0_xattn_all

    def _L0_ffn_setup():
        import jax, jax.numpy as jnp
        import numpy as np
        B, T, D, E, F, K, ND = (2, 64, 512, 64, 128, 4, 4)
        H = F * K
        N_SHARED = 2
        key = jax.random.key(seed)
        ks = jax.random.split(key, 12)
        s = lambda k, shape: jax.random.normal(k, shape, jnp.float32) * 0.02
        x = jax.random.normal(ks[0], (B, T, D), jnp.float32)
        Wr = s(ks[1], (E, D))
        router_bias = jnp.zeros((E,), jnp.float32)
        affinity = s(ks[2], (E, ND))
        te_W1 = s(ks[3], (D // 2, D))
        te_b1 = jnp.zeros((D // 2,), jnp.float32)
        te_W2 = s(ks[4], (ND, D // 2))
        te_b2 = jnp.zeros((ND,), jnp.float32)
        Wg = s(ks[5], (E, D, F))
        Wu = s(ks[6], (E, D, F))
        Wd = s(ks[7], (E, F, D))
        Sg = s(ks[8], (N_SHARED, D, H))
        Su = s(ks[9], (N_SHARED, D, H))
        Sd = s(ks[10], (N_SHARED, H, D))
        return dict(x=x, Wr=Wr, router_bias=router_bias, affinity=affinity, te_W1=te_W1, te_b1=te_b1, te_W2=te_W2, te_b2=te_b2, Wg=Wg, Wu=Wu, Wd=Wd, Sg=Sg, Su=Su, Sd=Sd)
    _L0_ffn_all = _L0_ffn_setup()
    _L0_ffn_in = {k: v for k, v in _L0_ffn_all.items() if k in ('Wr', 'router_bias', 'affinity', 'te_W1', 'te_b1', 'te_W2', 'te_b2', 'Wg', 'Wu', 'Wd', 'Sg', 'Su', 'Sd')}
    del _L0_ffn_all
    return {'x': x, 'ctx_1024': ctx_1024, 'g_xattn': g_xattn, 'g_ffn': g_ffn, 'L0_xattn_Wq': _L0_xattn_in['Wq'], 'L0_xattn_bq': _L0_xattn_in['bq'], 'L0_xattn_Wk': _L0_xattn_in['Wk'], 'L0_xattn_bk': _L0_xattn_in['bk'], 'L0_ffn_Wr': _L0_ffn_in['Wr'], 'L0_ffn_router_bias': _L0_ffn_in['router_bias'], 'L0_ffn_affinity': _L0_ffn_in['affinity'], 'L0_ffn_te_W1': _L0_ffn_in['te_W1'], 'L0_ffn_te_b1': _L0_ffn_in['te_b1'], 'L0_ffn_te_W2': _L0_ffn_in['te_W2'], 'L0_ffn_te_b2': _L0_ffn_in['te_b2'], 'L0_ffn_Wg': _L0_ffn_in['Wg'], 'L0_ffn_Wu': _L0_ffn_in['Wu'], 'L0_ffn_Wd': _L0_ffn_in['Wd'], 'L0_ffn_Sg': _L0_ffn_in['Sg'], 'L0_ffn_Su': _L0_ffn_in['Su'], 'L0_ffn_Sd': _L0_ffn_in['Sd']}

def reference(x, ctx_1024, g_xattn, g_ffn, L0_xattn_Wq, L0_xattn_bq, L0_xattn_Wk, L0_xattn_bk, L0_ffn_Wr, L0_ffn_router_bias, L0_ffn_affinity, L0_ffn_te_W1, L0_ffn_te_b1, L0_ffn_te_W2, L0_ffn_te_b2, L0_ffn_Wg, L0_ffn_Wu, L0_ffn_Wd, L0_ffn_Sg, L0_ffn_Su, L0_ffn_Sd):
    import jax
    import jax.numpy as jnp

    def _L0_xattn_ref(teacher_logits, teacher_features, Wq, bq, Wk, bk):
        import jax, jax.numpy as jnp
        import numpy as np
        query = jnp.einsum('bnc,dc->bnd', teacher_features, Wq) + bq
        key = jnp.einsum('bnc,dc->bnd', teacher_features, Wk) + bk
        energy = jnp.einsum('bnd,bmd->bnm', query, key)
        attention = jax.nn.softmax(energy, axis=-1)
        x_m = jnp.einsum('bln,bmn->blm', teacher_logits, attention)
        return x_m

    def _L0_ffn_ref(x, Wr, router_bias, affinity, te_W1, te_b1, te_W2, te_b2, Wg, Wu, Wd, Sg, Su, Sd):
        import jax, jax.numpy as jnp
        import numpy as np
        B, T, D, E, F, K, ND = (2, 64, 512, 64, 128, 4, 4)
        H = F * K
        N_SHARED = 2
        b, t, d = x.shape
        n = b * t
        flat = x.reshape(n, d)
        xm = x.mean(axis=1)
        h1 = jax.nn.gelu(xm @ te_W1.T + te_b1, approximate=False)
        task_dist = jax.nn.softmax(h1 @ te_W2.T + te_b2, axis=-1)
        dom = task_dist @ affinity.T
        logits = (flat @ Wr.T).reshape(b, t, E) + 0.5 * dom[:, None, :]
        logits = logits.reshape(n, E)
        scores = jax.nn.softmax(logits, axis=-1)
        _, topk_idx = jax.lax.top_k(logits + router_bias, K)
        topk_scores = jnp.take_along_axis(scores, topk_idx, axis=-1)
        topk_scores = topk_scores / (topk_scores.sum(-1, keepdims=True) + 1e-08)
        combine = jnp.zeros((n, E), x.dtype).at[jnp.arange(n)[:, None], topk_idx].add(topk_scores)
        g = jnp.einsum('nd,edf->enf', flat, Wg)
        u = jnp.einsum('nd,edf->enf', flat, Wu)
        h = jax.nn.silu(g) * u
        hw = h * combine.T[:, :, None]
        out = jnp.einsum('enf,efd->nd', hw, Wd)
        for i in range(Sg.shape[0]):
            sh = jax.nn.silu(flat @ Sg[i]) * (flat @ Su[i])
            out = out + sh @ Sd[i]
        return out.reshape(b, t, d)
    x = x + jnp.tanh(g_xattn[0]) * _L0_xattn_ref(_layernorm(x, axis=-1), ctx_1024, L0_xattn_Wq, L0_xattn_bq, L0_xattn_Wk, L0_xattn_bk)
    x = x + jnp.tanh(g_ffn[0]) * _L0_ffn_ref(_layernorm(x, axis=-1), L0_ffn_Wr, L0_ffn_router_bias, L0_ffn_affinity, L0_ffn_te_W1, L0_ffn_te_b1, L0_ffn_te_W2, L0_ffn_te_b2, L0_ffn_Wg, L0_ffn_Wu, L0_ffn_Wd, L0_ffn_Sg, L0_ffn_Su, L0_ffn_Sd)
    return x

_drawn_inputs = setup_inputs


def setup_inputs(seed=0):
    import zlib

    import numpy as np

    out = dict(_drawn_inputs(seed))
    spreads = {'L0_xattn_bq': (0.0, 0.1),
     'L0_xattn_bk': (0.0, 2.0),
     'L0_ffn_router_bias': (0.0, 0.8),
     'L0_ffn_te_b1': (0.0, 0.8),
     'L0_ffn_te_b2': (0.0, 2.0)}
    factors = {'L0_ffn_Wr': 5.659,
     'L0_ffn_affinity': 8.0,
     'L0_ffn_te_W1': 59.73,
     'L0_ffn_te_W2': 8.0,
     'L0_ffn_Wg': 5.477,
     'L0_ffn_Wu': 5.351,
     'L0_ffn_Wd': 5.342,
     'L0_ffn_Sg': 3.022,
     'L0_ffn_Su': 2.97,
     'L0_ffn_Sd': 2.966}
    for name, (base, spread) in spreads.items():
        noise = np.random.default_rng([zlib.crc32(name.encode()), seed]).standard_normal(out[name].shape)
        drawn = base * np.exp(spread * noise) if base else spread * noise
        out[name] = jnp.asarray(drawn.astype(out[name].dtype))
    for name, factor in factors.items():
        out[name] = (out[name] * factor).astype(out[name].dtype)
    return out
```

```python
import numpy as np
import concourse.bass as bass
from concourse import mybir
from contextlib import ExitStack

B, T, D, C, DK = 4, 512, 512, 256, 128
E, F, KTOP, ND, NSH = 64, 128, 4, 4, 2
NT = B * T // 128
NTILE = E + 63
PAR = {}


def _layout():
    at = 0
    for name, w in (("wq", 256), ("wk", 256), ("bqk", 2), ("g", 2), ("ident", 128), ("rb", 64), ("wr", 256),
                    ("te1", 1024), ("tb1", 2), ("te2", 8), ("tb2", 4), ("aff", 256), ("iota", 64),
                    ("iota128", 64), ("mean", 1), ("half", 128), ("tri", 128), ("one", 128), ("eps", 1)):
        PAR[name] = (at, at + w)
        at += w
    return at


PARW = _layout()


class Queues:

    def __init__(self, nc, ctx):
        self.nc, self.ctx = nc, ctx
        self.lists = {e: [] for e in ("pe", "act", "dve", "pool", "sp")}
        self.sems, self.count = {}, {}

    def sem(self, name):
        if name not in self.sems:
            self.sems[name] = self.ctx.enter_context(self.nc.semaphore(name))
            self.count[name] = 0
        return self.sems[name]

    def add(self, engine, f, waits=(), sig=None, by=1):
        waits = [w for w in waits if w is not None]
        out = None
        sem = None
        if sig is not None:
            sem = self.sem(sig)
            self.count[sig] += by
            out = (sig, self.count[sig])
        self.lists[engine].append(("op", f, waits, sem, by))
        return out

    def dma(self, engine, f, waits, sig):
        return self.add(engine, f, waits, sig, 16)

    def begin_if(self, engines, i):
        for e in engines:
            self.lists[e].append(("if", i))

    def end_if(self, engines):
        for e in engines:
            self.lists[e].append(("endif",))

    def play(self, name, eng, cond):
        todo = self.lists[name]
        seen = {}

        def run(at, local):
            while at < len(todo):
                item = todo[at]
                if item[0] == "op":
                    _, f, waits, sem, by = item
                    for s, v in waits:
                        if max(seen.get(s, 0), local.get(s, 0)) < v:
                            eng.wait_ge(self.sems[s], v)
                            local[s] = v
                    ins = f(eng)
                    if sem is not None:
                        ins.then_inc(sem, by)
                    at += 1
                elif item[0] == "if":
                    with eng.If(cond(eng, item[1])):
                        at = run(at + 1, dict(local))
                else:
                    return at + 1
            return at

        run(0, seen)


class Ring:

    def __init__(self, bufs):
        self.bufs, self.free, self.n = bufs, [()] * len(bufs), 0

    def take(self):
        i = self.n % len(self.bufs)
        self.n += 1
        return i, self.bufs[i], self.free[i]

    def give(self, i, *readers):
        self.free[i] = readers


def build(nc, x, ctxT, par, wsh, wex, tok, out):
    fp32, i32 = mybir.dt.float32, mybir.dt.int32
    u32 = mybir.dt.uint32
    ALU, ACT, AX = mybir.AluOpType, mybir.ActivationFunctionType, mybir.AxisListType
    ctx = ExitStack()
    with ctx:
        q = Queues(nc, ctx)
        add, dma = q.add, q.dma

        def sb(name, shape, dt=fp32):
            return ctx.enter_context(nc.sbuf_tensor(name, shape, dt))

        NW, NG, NYS = 5, 3, 3
        P_ = sb("par_sb", [128, PARW])

        def p(name, a=0, b=None):
            lo, hi = PAR[name]
            return P_[:, lo + a:(hi if b is None else lo + b)]

        acc = sb("acc", [128, NT, D])
        xT = sb("xT", [128, B, 4, T])
        shw = sb("shw", [128, NSH, 3, 4, 512])
        wall = sb("wall", [128, NW * 1536])
        W = [wall[:, 1536 * i:1536 * i + 1536] for i in range(NW)]
        xg = [sb(f"xg{i}", [128, D]) for i in range(NG)]
        work = sb("work", [128, 10 * 1024 // 4 * 4])
        small = sb("small", [128, 96])
        oh = wall[:, 1536:5632].rearrange("p (k j e) -> p k j e", k=4, j=NT)
        Msum = wall[:, 5632:6656].rearrange("p (j e) -> p j e", j=NT)
        Run = wall[:, 6656:7680].rearrange("p (j e) -> p j e", j=NT)
        cnt = wall[:, 0:512].rearrange("p (a e) -> p a e", a=8)
        tokid = sb("tokid", [128, NT], i32)
        table = sb("table", [128, 128], i32)
        eid = sb("eid", [1, 66], i32)

        def cut(t, a, shape):
            n = int(np.prod(shape))
            v = t[:, a:a + n]
            if len(shape) == 2:
                v = v.rearrange("p (a b) -> p a b", a=shape[0])
            return v

        cx = cut(work, 0, [2, 512])
        qs = cut(work, 1024, [512])
        ks = cut(work, 1536, [512])
        Am = cut(work, 2048, [4, 512])
        xn = cut(work, 4096, [4, 512])
        AT = cut(work, 6144, [4, 512])
        xnT = cut(work, 8192, [4, 512])
        hs = cut(work, 6144, [8, 512])
        ssil = [sb(f"ssil{i}", [128, 512]) for i in range(2)]
        xgT = [cut(work, 0 + 512 * i, [4, 128]) for i in range(2)]
        sg = [cut(work, 1024 + 128 * i, [128]) for i in range(2)]
        hh = [cut(work, 1280 + 128 * i, [128]) for i in range(2)]
        ysb = [cut(work, 1536 + 512 * i, [512]) for i in range(NYS)]
        yg = [cut(work, 3072 + 512 * i, [512]) for i in range(6)]

        bank = [ctx.enter_context(nc.psum_tensor(f"bank{i}", [128, 512], fp32)) for i in range(8)]

        xnd = nc.dram_tensor("xnd", (NT * 128, D), fp32)
        tabd = nc.dram_tensor("tabd", (128 * 128, 1), i32)
        yd = nc.dram_tensor("yd", (NTILE * 128, D), fp32)

        t_par = dma("sp", lambda e: e.dma_start(P_[:, :], par), (), "d_par")
        t_x, t_cx = {}, {}

        def load_x(b):
            t_x[b] = dma("sp", lambda e: e.dma_start(
                acc[:, 4 * b:4 * b + 4, :], x[b].rearrange("(c p) d -> p c d", p=128)), (), f"d_x{b}")

        def load_cx(b, waits):
            t_cx[b] = dma("sp", lambda e: e.dma_start(cx, ctxT[b]), waits, "d_cx")

        load_cx(0, ())
        load_x(0)
        load_x(1)
        t_tok = dma("act", lambda e: e.dma_start(tokid[:, :], tok), (), "d_tok")
        t_sh = [dma("act", lambda e, i=i: e.dma_start(shw[:, i, :, :, :], wsh[i]), (), f"d_sh{i}") for i in range(NSH)]
        load_x(2)
        load_x(3)
        t_z = add("dve", lambda e: e.memset(table[:, :], 0), (), "zero")
        t_tab0 = dma("act", lambda e: e.dma_start(
            tabd.ap().rearrange("(a b) o -> a (b o)", b=128), table[:, :]), [t_z], "d_tab0")
        t_zx = add("dve", lambda e: e.memset(xg[0][:, :], 0.0), (), "zero")
        t_zy = []
        for n in range(3):
            t_zy.append(dma("act", lambda e, n=n: e.dma_start(
                yd.ap()[128 * (E + 21 * n):128 * (E + 21 * n + 21), :].rearrange("(t p) d -> p t d", p=128),
                xg[0][:, :].unsqueeze(1).to_broadcast([128, 21, D])), [t_zx], f"d_zy{n}"))
        t_tanh = add("act", lambda e: e.activation(small[:, 0:2], p("g"), ACT.Tanh), [t_par], "tanh")
        tg1, tg2 = small[:, 0:1], small[:, 1:2]

        banks = Ring(bank)

        def pe(f, waits=(), sig=None):
            return add("pe", f, waits, sig)

        def group(ms, waits, sig):
            t = None
            for n, (o, l, r, s0, s1) in enumerate(ms):
                t = pe(lambda e, o=o, l=l, r=r, s0=s0, s1=s1: e.matmul(o, l, r, start=s0, stop=s1),
                       waits if n == 0 else (), sig if n == len(ms) - 1 else None)
            return t

        def transposes(ms, waits, sig):
            t = None
            for n, (o, i) in enumerate(ms):
                t = pe(lambda e, o=o, i=i: e.transpose(o, i, p("ident")), waits if n == 0 else (),
                       sig if n == len(ms) - 1 else None)
            return t

        turn = [0]

        def evac(o, i, waits, sig):
            turn[0] += 1
            if turn[0] % 2:
                return add("act", lambda e: e.activation(o, i, ACT.Copy), waits, sig + "_a")
            return add("dve", lambda e: e.tensor_copy(o, i), waits, sig + "_v")

        stats = sb("stats", [128, 4, 6])
        mv = sb("mv", [128, 4, 2])
        rs = sb("rs", [128, 4])
        sd = sb("sd", [128, 4])
        mx = sb("mx", [128, 4])
        nmx = sb("nmx", [128, 4])
        sm = sb("sm", [128, 4])
        ri = sb("ri", [128, 4])

        def layernorm(b, ready, free):
            done = []
            for c in range(4):
                src = acc[:, 4 * b + c, :]
                t = add("dve", lambda e, c=c, src=src: e.bn_stats(stats[:, c, :], src), [ready[c]], "ln")
                t = add("dve", lambda e, c=c: e.bn_aggr(mv[:, c, :], stats[:, c, :]), [t], "ln")
            t = add("act", lambda e: e.activation(sd[:, :], mv[:, :, 1], ACT.Sqrt, bias=p("eps")), [t, t_par], "sd")
            t = add("dve", lambda e: e.reciprocal(rs[:, :], sd[:, :]), [t], "ln")
            for c in range(4):
                src = acc[:, 4 * b + c, :]
                done.append(add("dve", lambda e, c=c, src=src: e.tensor_scalar(
                    xn[:, c, :], src, mv[:, c, 0:1], rs[:, c:c + 1], ALU.subtract, ALU.mult),
                    [t, *(free if c == 0 else ())], "ln"))
            return done

        st = {"xn_free": (), "at_free": (), "xnT_free": (), "qk_free": None, "xT": {}, "xnd": []}

        def attention(b):
            ln = layernorm(b, [t_x[b]] * 4, st["xn_free"])
            i0, pq, f0 = banks.take()
            tq = group([(pq[:, :], p("wq", 128 * c, 128 * c + 128), cx[:, c, :], c == 0, c == 1) for c in range(2)],
                       [t_par, t_cx[b], *f0], "qk")
            i1, pk, f1 = banks.take()
            tk = group([(pk[:, :], p("wk", 128 * c, 128 * c + 128), cx[:, c, :], c == 0, c == 1) for c in range(2)],
                       [*f1], "qk")
            st["cx_free"] = tk
            if b + 1 < B:
                load_cx(b + 1, [tk])
            tq = add("act", lambda e: e.activation(qs, pq[:, :], ACT.Identity, bias=p("bqk", 0, 1)),
                     [tq, st["qk_free"]], "qs")
            tk = add("dve", lambda e: e.tensor_scalar(ks, pk[:, :], p("bqk", 1, 2), None, ALU.add),
                     [tk, st["qk_free"]], "ks")
            banks.give(i0, tq)
            banks.give(i1, tk)
            te = []
            for m in range(4):
                i, pb, f = banks.take()
                t = group([(pb[:, :], qs[:, 128 * m:128 * m + 128], ks, True, True)], [tq, tk, *f], "en")
                st["qk_free"] = t
                t1 = add("dve", lambda e, m=m, pb=pb: e.reduce_max(mx[:, m:m + 1], pb[:, :], AX.X), [t], "mx")
                t1 = add("dve", lambda e, m=m: e.tensor_scalar(nmx[:, m:m + 1], mx[:, m:m + 1], -1.0, None, ALU.mult),
                         [t1, st.get(("exp", m))], "mx")
                t2 = add("act", lambda e, m=m, pb=pb: e.activation(
                    Am[:, m, :], pb[:, :], ACT.Exp, bias=nmx[:, m:m + 1], accum_out=sm[:, m:m + 1]),
                    [t1, *(st["at_free"] if m == 0 else ())], "exp")
                st[("exp", m)] = t2
                banks.give(i, t2)
                t3 = add("dve", lambda e, m=m: e.reciprocal(ri[:, m:m + 1], sm[:, m:m + 1]), [t2], "at")
                t3 = add("dve", lambda e, m=m: e.tensor_scalar(Am[:, m, :], Am[:, m, :], ri[:, m:m + 1], None,
                                                               ALU.mult), [t3], "at")
                te.append(t3)
            txT = []
            for n in range(4):
                i, pb, f = banks.take()
                t = transposes([(pb[:, 128 * c:128 * c + 128], xn[:, c, 128 * n:128 * n + 128]) for c in range(4)],
                               [*ln, *f], "tr")
                st["xn_free"] = (t,)
                t = evac(xnT[:, n, :], pb[:, :], [t, *st["xnT_free"]], "xnT")
                banks.give(i, t)
                txT.append(t)
            tAT = []
            for n in range(4):
                i, pb, f = banks.take()
                t = transposes([(pb[:, 128 * m:128 * m + 128], Am[:, m, 128 * n:128 * n + 128]) for m in range(4)],
                               [*te, *f], "tr")
                st["at_free"] = (t,)
                t = evac(AT[:, n, :], pb[:, :], [t, *st["xnT_free"]], "AT")
                banks.give(i, t)
                tAT.append(t)
            tx = []
            for c in range(4):
                i, pb, f = banks.take()
                t = group([(pb[:, :], xnT[:, n, 128 * c:128 * c + 128], AT[:, n, :], n == 0, n == 3)
                           for n in range(4)], [*txT, *tAT, *f], "xm")
                st["xnT_free"] = (t,)
                a = acc[:, 4 * b + c, :]
                t = add("dve", lambda e, a=a, pb=pb: e.scalar_tensor_tensor(a, pb[:, :], tg1, a, ALU.mult, ALU.add),
                        [t, t_tanh], "x1")
                banks.give(i, t)
                tx.append(t)
            st[("x1", b)] = tx

        def second_norm(b):
            ln = layernorm(b, st[("x1", b)], st["xn_free"])
            t = dma("sp", lambda e: e.dma_start(
                xnd.ap()[512 * b:512 * b + 512, :].rearrange("(c p) d -> p c d", p=128), xn), ln, f"d_xn{b}")
            st["xnd"].append(t)
            st["store"] = t
            out_t = []
            for c in range(4):
                i, pb, f = banks.take()
                tp = transposes([(pb[:, 128 * k:128 * k + 128], xn[:, c, k:512:4]) for k in range(4)],
                                [*ln, *f], "tr")
                tt = evac(xT[:, b, :, 128 * c:128 * c + 128], pb[:, :].rearrange("p (k t) -> p k t", k=4), [tp], "xT")
                banks.give(i, tt)
                out_t.append(tt)
            i, pb, f = banks.take()
            tm = group([(pb[:, k:k + 1], xn[:, c, k:512:4], p("mean"), c == 0, c == 3)
                        for k in range(4) for c in range(4)], [*f], "xm1")
            st["xn_free"] = (tm, t)
            tm2 = add("dve", lambda e: e.tensor_copy(small[:, 4 + 4 * b:8 + 4 * b], pb[:, 0:4]), [tm], "xms")
            banks.give(i, tm2)
            st["xT"][b] = out_t
            st[("xm", b)] = tm2

        def task_hidden(b):
            i, pb, f = banks.take()
            te1 = p("te1").rearrange("p (k j) -> p k j", k=4)
            t = group([(pb[:, j:j + 1], te1[:, k, 128 * j:128 * j + 128], small[:, 4 + 4 * b + k:5 + 4 * b + k],
                        k == 0, k == 3) for j in range(2) for k in range(4)], [st[("xm", b)], *f], "h1")
            for j in range(2):
                t1 = add("act", lambda e, j=j: e.activation(small[:, 20 + 2 * b + j:21 + 2 * b + j], pb[:, j:j + 1],
                                                            ACT.Gelu, bias=p("tb1", j, j + 1)), [t], "gelu")
            banks.give(i, t1)
            st[("h1", b)] = t1

        row = sb("row", [1, 4, 80])

        def task_dist(b):
            i, pb, f = banks.take()
            te2 = p("te2").rearrange("p (j n) -> p j n", j=2)
            t = group([(pb[0:1, 0:4], small[:, 20 + 2 * b + j:21 + 2 * b + j], te2[:, j, :], j == 0, j == 1)
                       for j in range(2)], [st[("h1", b)], *f], "l2")
            r = row[:, b, :]
            t = add("dve", lambda e: e.tensor_tensor(r[:, 0:4], pb[0:1, 0:4], p("tb2")[0:1, :], ALU.add), [t], "td")
            banks.give(i, t)
            t = add("dve", lambda e: e.reduce_max(r[:, 8:9], r[:, 0:4], AX.X), [t], "td")
            t = add("dve", lambda e: e.tensor_scalar(r[:, 9:10], r[:, 8:9], -1.0, None, ALU.mult), [t], "td")
            t = add("act", lambda e: e.activation(r[:, 4:8], r[:, 0:4], ACT.Exp, bias=r[:, 9:10],
                                                  accum_out=r[:, 10:11]), [t], "tde")
            t = add("dve", lambda e: e.reciprocal(r[:, 11:12], r[:, 10:11]), [t], "td")
            t = add("dve", lambda e: e.tensor_scalar(r[:, 12:16], r[:, 4:8], r[:, 11:12], None, ALU.mult), [t], "td")
            d = r[:, 16:80]
            aff = p("aff").rearrange("p (n e) -> p n e", n=4)
            t = add("dve", lambda e: e.tensor_scalar(d, aff[0:1, 0, :], r[:, 12:13], None, ALU.mult), [t], "td")
            for n in range(1, 4):
                t = add("dve", lambda e, n=n: e.scalar_tensor_tensor(d, aff[0:1, n, :], r[:, 12 + n:13 + n], d,
                                                                     ALU.mult, ALU.add), [t], "td")
            st[("dom", b)] = t

        lg, lb, ex, tmp = (cut(work, 256 * n, [4, E]) for n in range(4))
        v8 = sb("v8", [128, 4, 8])
        i8 = sb("i8", [128, 4, 8], u32)
        i8f = sb("i8f", [128, 4, 8])
        rmx = sb("rmx", [128, 4])
        Zs = sb("Zs", [128, NT])
        Es = sb("Es", [128, 4, NT])

        def bc(ap, shape):
            return ap.to_broadcast(shape)

        def router(b):
            i, pb, f = banks.take()
            wr = p("wr").rearrange("p (k e) -> p k e", k=4)
            ms = []
            for c in range(4):
                o = pb[:, 64 * c:64 * c + 64]
                ms += [(o, xT[:, b, k, 128 * c:128 * c + 128], wr[:, k, :], k == 0, False) for k in range(4)]
                ms += [(o, p("half")[0:1, :], row[:, b, 16:80], False, True)]
            t = group(ms, [*st["xT"][b], st[("dom", b)], *f], "lg")
            t = add("dve", lambda e: e.tensor_copy(lg[:, :, :], pb[:, 0:256].rearrange("p (c e) -> p c e", c=4)),
                    [t, st.get("exr"), st["cx_free"]], "rt")
            banks.give(i, t)
            t0 = add("dve", lambda e: e.tensor_tensor(lb[:, :, :], lg[:, :, :],
                                                     bc(p("rb").unsqueeze(1), [128, 4, E]), ALU.add), [t], "rt")
            t = add("dve", lambda e: e.tensor_reduce(rmx[:, :], lg[:, :, :], AX.X, ALU.max), [t], "rt")
            t = add("dve", lambda e: e.tensor_tensor(tmp[:, :, :], lg[:, :, :],
                                                     bc(rmx[:, :].unsqueeze(2), [128, 4, E]), ALU.subtract),
                    [t], "rt")
            tex = add("act", lambda e: e.activation(ex[:, :, :], tmp[:, :, :], ACT.Exp), [t], "rexp")
            for c in range(4):
                t = add("dve", lambda e, c=c: e.max(v8[:, c, :], lb[:, c, :]), [t0], "rt")
                t = add("dve", lambda e, c=c: e.max_index(i8[:, c, :], v8[:, c, :], lb[:, c, :]), [t], "rt")
            t = add("dve", lambda e: e.tensor_copy(i8f[:, :, :], i8[:, :, :]), [t], "rt")
            for k in range(4):
                o = oh[:, k, 4 * b:4 * b + 4, :]
                to = add("dve", lambda e, k=k, o=o: e.tensor_tensor(
                    o, bc(p("iota").unsqueeze(1), [128, 4, E]), bc(i8f[:, :, k:k + 1], [128, 4, E]), ALU.is_equal),
                    [t], "rt")
                st[("oh", b, k)] = to
            M = Msum[:, 4 * b:4 * b + 4, :]

            def o(k):
                return oh[:, k, 4 * b:4 * b + 4, :]
            t = add("dve", lambda e: e.tensor_tensor(M, o(0), o(1), ALU.add), [to], "rt")
            t = add("dve", lambda e: e.tensor_tensor(M, M, o(2), ALU.add), [t], "rt")
            t = add("dve", lambda e: e.tensor_tensor(M, M, o(3), ALU.add), [t], "rt")
            st[("M", b)] = t
            for c in range(4):
                j = 4 * b + c
                if j == 0:
                    t = add("dve", lambda e: e.memset(Run[:, 0, :], 0.0), (), "rt")
                else:
                    t = add("dve", lambda e, j=j: e.tensor_tensor(Run[:, j, :], Run[:, j - 1, :], Msum[:, j - 1, :],
                                                                  ALU.add), [t], "rt")
            st[("R", b)] = t
            t = add("dve", lambda e: e.tensor_reduce(Zs[:, 4 * b:4 * b + 4], ex[:, :, :], AX.X, ALU.add), [tex], "rt")
            for k in range(4):
                t = add("dve", lambda e, k=k: e.tensor_tensor(tmp[:, :, :], o(k), ex[:, :, :], ALU.mult), [t], "rt")
                t = add("dve", lambda e, k=k: e.tensor_reduce(Es[:, k, 4 * b:4 * b + 4], tmp[:, :, :], AX.X, ALU.add),
                        [t], "rt")
            st["exr"] = t

        slot = cut(work, 0, [4, NT])
        sloti = sb("sloti", [128, 4, NT], i32)
        addr = sb("addr", [128, 4, NT], i32)
        ai = work[:, 64:128].bitcast(i32).rearrange("p (a b) -> p a b", a=4)
        cni = cnt[:, 6:8, :].bitcast(i32)
        wts = sb("wts", [128, 4, NT])
        wz = cut(work, 128, [4, NT])

        def dispatch():
            i2, pc, f2 = banks.take()
            tc = group([(pc[:, 0:64], p("one"), Run[:, NT - 1, :], True, False),
                        (pc[:, 0:64], p("one"), Msum[:, NT - 1, :], False, True)],
                       [st[("R", B - 1)], st[("M", B - 1)], *f2], "pos")
            ps = []
            for half in range(2):
                i, pb, f = banks.take()
                ms = []
                for j in range(8 * half, 8 * half + 8):
                    o = pb[:, 64 * (j % 8):64 * (j % 8) + 64]
                    ms += [(o, p("tri"), Msum[:, j, :], True, False), (o, p("one"), Run[:, j, :], False, True)]
                ps.append((i, pb, group(ms, [*f], "pos")))
            st["pos"] = ps[1][2]
            t = add("dve", lambda e: e.tensor_scalar(cni[:, 0, :], pc[:, 0:64], -1.0, None, ALU.add), [tc], "dp")
            banks.give(i2, t)
            t = add("dve", lambda e: e.tensor_scalar(cni[:, 1, :], cni[:, 0, :], 7, None, ALU.arith_shift_right),
                    [t], "dp")
            t = add("dve", lambda e: e.tensor_scalar(cnt[:, 0, :], cni[:, 1, :], 0.0, None, ALU.max), [t], "dp")
            src, step = 0, 1
            while step < 64:
                dst = 1 if src != 1 else 2
                add("dve", lambda e, s=src, d=dst, n=step: e.tensor_copy(cnt[:, d, 0:n], cnt[:, s, 0:n]), [t], "dp")
                t = add("dve", lambda e, s=src, d=dst, n=step: e.tensor_tensor(
                    cnt[:, d, n:64], cnt[:, s, n:64], cnt[:, s, 0:64 - n], ALU.add), [t], "dp")
                src, step = dst, 2 * step
            incl = src
            t1 = add("dve", lambda e: e.tensor_tensor(cnt[:, 3, :], cnt[:, incl, :], cnt[:, 0, :], ALU.subtract),
                     [t], "dp")
            t1 = add("dve", lambda e: e.tensor_scalar(cnt[:, 4, :], cnt[:, 3, :], 63.0, 128.0, ALU.add, ALU.mult),
                     [t1], "dp")
            t1 = add("dve", lambda e: e.tensor_tensor(cnt[:, 5, :], cnt[:, 4, :], p("iota128"), ALU.subtract),
                     [t1], "dp")
            slotd = xn_slot
            for half, (i, pb, tp) in enumerate(ps):
                v = pb[:, :].rearrange("p (j e) -> p j e", j=8)
                o = slotd[:, 8 * half:8 * half + 8, :]
                t2 = add("dve", lambda e, o=o, v=v: e.tensor_scalar(o, v, 128.0, None, ALU.is_ge), [tp, t1, *xn_free()],
                         "dp")
                t2 = add("dve", lambda e, o=o: e.tensor_tensor(o, o, bc(cnt[:, 5:6, :], [128, 8, E]), ALU.mult),
                         [t2], "dp")
                t2 = add("dve", lambda e, o=o, v=v: e.tensor_tensor(o, o, v, ALU.add), [t2], "dp")
                banks.give(i, t2)
                t2 = add("dve", lambda e, o=o: e.tensor_tensor(o, o, bc(p("iota128").unsqueeze(1), [128, 8, E]),
                                                               ALU.add), [t2], "dp")
            for k in range(4):
                t3 = add("dve", lambda e, k=k: e.tensor_tensor(oh[:, k, :, :], oh[:, k, :, :], slotd[:, :, :],
                                                               ALU.mult), [t2], "dp")
                t3 = add("dve", lambda e, k=k: e.tensor_reduce(slot[:, k, :], oh[:, k, :, :], AX.X, ALU.add),
                         [t3], "dp")
            t4 = add("dve", lambda e: e.tensor_copy(sloti[:, :, :], slot[:, :, :]), [t3], "dp")
            st["slots"] = t4
            ta = add("dve", lambda e: e.tensor_scalar(ai[:, :, :], sloti[:, :, :], 127, 7, ALU.bitwise_and,
                                                      ALU.logical_shift_left), [t4], "dp")
            tb = add("dve", lambda e: e.tensor_scalar(addr[:, :, :], sloti[:, :, :], 7, None,
                                                      ALU.logical_shift_right), [t4], "dp")
            tb = add("dve", lambda e: e.tensor_tensor(addr[:, :, :], addr[:, :, :], ai[:, :, :], ALU.bitwise_or),
                     [ta, tb], "dp")
            tsc = []
            for j in range(NT):
                for k in range(4):
                    tsc.append(dma("pool", lambda e, j=j, k=k: e.indirect_dma_start(
                        tabd.ap()[:, :], bass.IndirectOffsetOnAxis(ap=addr[:, k, j:j + 1], axis=0),
                        tokid[:, j:j + 1], None), [tb, t_tab0, t_tok], "d_sc"))
            st["table"] = dma("pool", lambda e: e.dma_start(
                table[:, :], tabd.ap().rearrange("(a b) o -> a (b o)", b=128)), [tsc[-1]], "d_tab")
            cmpv = cut(work, 2048, [64, 64])[0:1]
            t5 = add("dve", lambda e: e.tensor_tensor(
                cmpv, bc(cnt[0:1, incl:incl + 1, :], [1, 64, 64]),
                bc(p("iota")[0:1, :].unsqueeze(2), [1, 64, 64]), ALU.is_le), [t, *st["at_free"], *st["xn_free"]], "dp")
            t5 = add("dve", lambda e: e.tensor_reduce(row[:, 0, 0:64], cmpv, AX.X, ALU.add), [t5], "dp")
            add("dve", lambda e: e.tensor_copy(eid[:, 64:65], cnt[0:1, incl, 63:64]), [t5], "dp")
            st["eid"] = add("dve", lambda e: e.tensor_scalar(eid[:, 0:64], row[:, 0, 0:64], 63.0, None, ALU.min),
                            [t5], "dp")
            t6 = add("dve", lambda e: e.reciprocal(wz[:, 0, :], Zs[:, :]), [st["exr"]], "dw")
            for k in range(4):
                t6 = add("dve", lambda e, k=k: e.tensor_tensor(wts[:, k, :], Es[:, k, :], wz[:, 0, :], ALU.mult),
                         [t6], "dw")
            t6 = add("dve", lambda e: e.tensor_tensor(wz[:, 1, :], wts[:, 0, :], wts[:, 1, :], ALU.add), [t6], "dw")
            t6 = add("dve", lambda e: e.tensor_tensor(wz[:, 1, :], wz[:, 1, :], wts[:, 2, :], ALU.add), [t6], "dw")
            t6 = add("dve", lambda e: e.tensor_tensor(wz[:, 1, :], wz[:, 1, :], wts[:, 3, :], ALU.add), [t6], "dw")
            t6 = add("dve", lambda e: e.tensor_scalar(wz[:, 1, :], wz[:, 1, :], 1e-8, None, ALU.add), [t6], "dw")
            t6 = add("dve", lambda e: e.reciprocal(wz[:, 2, :], wz[:, 1, :]), [t6], "dw")
            t6 = add("dve", lambda e: e.tensor_scalar(wz[:, 2, :], wz[:, 2, :], tg2, None, ALU.mult),
                     [t6, t_tanh], "dw")
            for k in range(4):
                t6 = add("dve", lambda e, k=k: e.tensor_tensor(wts[:, k, :], wts[:, k, :], wz[:, 2, :], ALU.mult),
                         [t6], "dw")
            st["wts"] = t6

        xn_slot = cut(work, 1024, [16, 64])

        def xn_free():
            return (st["qk_free"],)

        shared = {"banks": banks, "free_h": {}, "h": {}, "sil": Ring(ssil), "n": 0}

        def up_piece(b, s, c):
            R = shared["banks"]
            i0, pg, f0 = R.take()
            i1, pu, f1 = R.take()
            hc = slice(128 * c, 128 * c + 128)
            w0 = [*st["xT"][b], t_sh[s]]
            tg_ = group([(pg[:, :], shw[:, s, 0, k, hc], xT[:, b, k, :], k == 0, k == 3) for k in range(4)],
                        [*w0, *f0], "sh")
            tu = group([(pu[:, :], shw[:, s, 1, k, hc], xT[:, b, k, :], k == 0, k == 3) for k in range(4)],
                       [*f1], "sh")
            si, sbuf, sf = shared["sil"].take()
            ts = add("act", lambda e: e.activation(sbuf[:, :], pg[:, :], ACT.Silu), [tg_, *sf], "silu")
            R.give(i0, ts)
            n = 4 * s + c
            th = add("dve", lambda e: e.tensor_tensor(hs[:, n, :], sbuf[:, :], pu[:, :], ALU.mult),
                     [ts, tu, *shared["free_h"].get(n, st["xnT_free"])], "hs")
            R.give(i1, th)
            shared["sil"].give(si, th)
            shared["h"][n] = th

        def down_piece(b, tc):
            R = shared["banks"]
            i, pb, f = R.take()
            t = group([(pb[:, :], hs[:, n, 128 * tc:128 * tc + 128], shw[:, n // 4, 2, n % 4, :], n == 0, n == 7)
                       for n in range(8)], [*shared["h"].values(), *f], "sh")
            if tc == 3:
                shared["free_h"] = {n: (t,) for n in range(8)}
            a = acc[:, 4 * b + tc, :]
            t = add("dve", lambda e: e.scalar_tensor_tensor(a, pb[:, :], tg2, a, ALU.mult, ALU.add),
                    [t, t_tanh, *st[("x1", b)]], "shacc")
            R.give(i, t)
            st[("shacc", 4 * b + tc)] = t

        pieces = []
        for b in range(B):
            pieces += [lambda b=b, s=s, c=c: up_piece(b, s, c) for s in range(NSH) for c in range(4)]
            pieces += [lambda b=b, tc=tc: down_piece(b, tc) for tc in range(4)]

        def piece(n=1):
            for _ in range(n):
                if pieces:
                    pieces.pop(0)()

        attention(0)
        attention(1)
        second_norm(0)
        attention(2)
        task_hidden(0)
        second_norm(1)
        attention(3)
        task_dist(0)
        task_hidden(1)
        second_norm(2)
        piece()
        router(0)
        task_dist(1)
        task_hidden(2)
        second_norm(3)
        piece()
        router(1)
        task_dist(2)
        task_hidden(3)
        piece()
        router(2)
        task_dist(3)
        piece()
        router(3)
        piece()
        dispatch()
        piece(7)
        piece(2)

        ENG = ("pe", "act", "dve", "pool", "sp")
        last = {}
        for i, r in enumerate(banks.free):
            last[i] = r
        sbanks = Ring([bank[0], bank[1]])
        sbanks.free = [last[0], last[1]]
        shared["banks"] = sbanks
        xtb = Ring([bank[2], bank[3]])
        gub = Ring([bank[4], bank[5]])
        yb = Ring([bank[6], bank[7]])
        for r, a in ((xtb, 2), (gub, 4), (yb, 6)):
            r.free = [last[a], last[a + 1]]
        tabs_read = st["pos"]
        stage_free = [*st["xnT_free"], *st["at_free"], *st["xn_free"], st["qk_free"], st["slots"], st["eid"], st["wts"], t_cx[B - 1]]
        tT, tG, tY, tW, tX, tEx, tEy, tYd = {}, {}, {}, {}, {}, {}, {}, {}
        tS, tH = {}, {}

        def load_weights(t):
            w = W[t % NW]
            waits = [tY.get(t - NW), *((st["slots"], st["eid"], tabs_read) if t < NW else ())]
            if t < E:
                tW[t] = dma("sp", lambda e: e.dma_start(w, wex[t]), waits, f"d_w{t % NW}")
            else:
                def f(e):
                    r = e.value_load(eid[0:1, t - E:t - E + 1], min_val=0, max_val=E - 1)
                    return e.dma_start(w, wex[bass.ds(r, 1), :, :].rearrange("o p n -> (o p) n"))
                tW[t] = dma("sp", f, [*waits, st["eid"]], f"d_w{t % NW}")

        def gather(t):
            tX[t] = dma("pool", lambda e: e.indirect_dma_start(
                xg[t % NG][:, :], None, xnd.ap()[:, :], bass.IndirectOffsetOnAxis(ap=table[:, t:t + 1], axis=0)),
                [st["table"], *st["xnd"], tT.get(t - NG), *(t_zy if t == 0 else ())], f"d_g{t % NG}")

        def turn_tile(t):
            i, pb, f = xtb.take()
            g = xg[t % NG]
            tT[t] = transposes([(pb[:, 128 * k:128 * k + 128], g[:, k:512:4]) for k in range(4)],
                               [tX[t], *f], "eT")
            o = xgT[t % 2]
            tEx[t] = add("act", lambda e: e.activation(o, pb[:, :].rearrange("p (k t) -> p k t", k=4), ACT.Copy),
                         [tT[t], tG.get(t - 2), *(stage_free if t < 2 else ())], "eX")
            xtb.give(i, tEx[t])

        def up_tile(t):
            i, pb, f = gub.take()
            w, xx = W[t % NW], xgT[t % 2]
            tG[t] = group([(pb[:, 128 * m:128 * m + 128], w[:, 512 * m + 128 * k:512 * m + 128 * k + 128], xx[:, k, :],
                            k == 0, k == 3) for m in range(2) for k in range(4)], [tW[t], tEx[t], *f], "eG")
            s, h = sg[t % 2], hh[t % 2]
            tS[t] = add("act", lambda e: e.activation(s, pb[:, 0:128], ACT.Silu), [tG[t], tH.get(t - 2), *(stage_free if t < 2 else ())], "eS")
            tH[t] = add("dve", lambda e: e.tensor_tensor(h, s, pb[:, 128:256], ALU.mult), [tS[t], tY.get(t - 2)],
                        "eH")
            gub.give(i, tH[t])

        def down_tile(t):
            i, pb, f = yb.take()
            w = W[t % NW]
            tY[t] = group([(pb[:, :], hh[t % 2], w[:, 1024:1536], True, True)], [tH[t], *f], "eY")
            o = ysb[t % NYS]
            tEy[t] = add("dve", lambda e: e.tensor_copy(o, pb[:, :]), [tY[t], tYd.get(t - NYS),
                                                                         *(stage_free if t < 2 else ())], "eE")
            yb.give(i, tEy[t])
            tYd[t] = dma("sp", lambda e: e.dma_start(yd.ap()[128 * t:128 * t + 128, :], o), [tEy[t], *(t_zy if t == E else ())],
                         f"d_y{t % NYS}")

        for t in range(NW - 1):
            load_weights(t)
        for t in range(NG):
            gather(t)
        turn_tile(0)
        conds = {}

        def cond(eng, i):
            if id(eng) not in conds:
                conds[id(eng)] = eng.value_load(eid[0:1, 64:65], min_val=0, max_val=63)
            return conds[id(eng)] > i - 1

        def iteration(i):
            if i + 1 < NTILE:
                turn_tile(i + 1)
            if i < NTILE:
                up_tile(i)
            if 1 <= i and i - 2 + NW < NTILE:
                load_weights(i - 2 + NW)
            if i + NG < NTILE:
                gather(i + NG)

        for i in range(NTILE + 1):
            dyn = i > E
            if dyn and (i - E) % 4 == 1 and i < E + 32:
                piece()
            if i == E + 1:
                for e in ENG:
                    q.add(e, lambda eng: conds.setdefault(id(eng), eng.value_load(
                        eid[0:1, 64:65], min_val=0, max_val=63)), [st["eid"]])
            if dyn:
                q.begin_if(ENG, i - E)
            iteration(i)
            if not dyn and i % 4 == 3:
                piece()
            if i >= 1:
                down_tile(i - 1)
            if i >= E:
                for t in ((i - 3, i - 2, i - 1) if i == E else (i - 1,)):
                    q.add("sp", lambda e: None, [tYd[t]])
            if dyn:
                q.end_if(ENG)

        t_all = add("sp", lambda e: e.nop(), (), "yall")
        ra = add("act", lambda e: e.activation(small[:, 80:81], small[:, 0:1], ACT.Copy), (), "endA")
        rv = add("dve", lambda e: e.tensor_copy(small[:, 81:82], small[:, 0:1]), (), "endV")
        fb = Ring(bank)
        fb.free = [*sbanks.free] + [(ra, rv)] * 6
        shared["banks"] = fb
        ygr = Ring(yg)
        tg_ = {}

        def fetch(j, k):
            i, g, f = ygr.take()
            t = dma("pool", lambda e: e.indirect_dma_start(
                g, None, yd.ap()[:, :], bass.IndirectOffsetOnAxis(ap=sloti[:, k, j:j + 1], axis=0)),
                [t_all, *f], f"d_yg{i}")
            tg_[(j, k)] = (i, g, t)

        def combine(j):
            for k in range(4):
                i, g, t = tg_[(j, k)]
                a = acc[:, j, :]
                t = add("dve", lambda e, a=a, g=g, k=k: e.scalar_tensor_tensor(a, g, wts[:, k, j:j + 1], a, ALU.mult,
                                                                                ALU.add),
                        [t, st["wts"], st[("shacc", j)] if k == 0 else last_c[0]], "comb")
                last_c[0] = t
                ygr.give(i, t)
            st[("comb", j)] = last_c[0]

        last_c = [None]
        outs = []

        def store(j):
            outs.append(dma("sp", lambda e: e.dma_start(out[j // 4, 128 * (j % 4):128 * (j % 4) + 128, :],
                                                        acc[:, j, :]), [st[("comb", j)]], "d_out"))

        for j in range(12):
            for k in range(4):
                fetch(j, k)
            combine(j)
            store(j)
            if len(pieces) > 4:
                piece()
        for j in range(12, 16):
            for k in range(4):
                fetch(j, k)
            piece()
            combine(j)
            store(j)
        assert not pieces
        q.add("sp", lambda e: None, [outs[-1]])

        block = ctx.enter_context(nc.Block())

        @block.sync
        def _(e):
            q.play("sp", e, cond)

        @block.gpsimd
        def _(e):
            q.play("pool", e, cond)

        @block.scalar
        def _(e):
            q.play("act", e, cond)

        @block.vector
        def _(e):
            q.play("dve", e, cond)

        @block.tensor
        def _(e):
            q.play("pe", e, cond)


def kernel(**inputs):
    import concourse.bacc as _bacc
    from concourse.bass_utils import run_bass_kernel_spmd as _run

    a = {k: np.asarray(v) for k, v in inputs.items()}
    f = np.float32
    par = np.zeros((128, PARW), f)

    def put(name, v):
        lo, hi = PAR[name]
        par[:, lo:hi] = np.broadcast_to(v, (128, hi - lo))

    def rows(m, k):
        return m.reshape(k, 128, -1).transpose(1, 0, 2).reshape(128, -1)

    put("wq", rows(a["L0_xattn_Wq"].T, 2))
    put("wk", rows(a["L0_xattn_Wk"].T, 2))
    put("bqk", np.stack([a["L0_xattn_bq"], a["L0_xattn_bk"]], 1))
    put("g", np.array([a["g_xattn"][0], a["g_ffn"][0]])[None])
    put("ident", np.eye(128, dtype=f))
    put("rb", a["L0_ffn_router_bias"][None])
    put("wr", a["L0_ffn_Wr"].T.reshape(128, 256))
    put("te1", a["L0_ffn_te_W1"].T.reshape(128, 1024))
    put("tb1", a["L0_ffn_te_b1"].reshape(2, 128).T)
    put("te2", rows(a["L0_ffn_te_W2"].T, 2))
    put("tb2", a["L0_ffn_te_b2"][None])
    put("aff", a["L0_ffn_affinity"].T.reshape(1, 256))
    put("iota", np.arange(64, dtype=f)[None])
    put("iota128", 128 * np.arange(64, dtype=f)[None])
    put("mean", np.full((1, 1), 1 / 512, f))
    put("half", np.full((1, 128), 0.5, f))
    put("tri", np.triu(np.ones((128, 128), f), 1))
    put("one", np.ones((1, 128), f))
    put("eps", np.full((1, 1), 1e-5, f))
    ctxT = np.ascontiguousarray(a["ctx_1024"].transpose(0, 2, 1).reshape(4, 2, 128, 512).transpose(0, 2, 1, 3))
    Sg, Su, Sd = a["L0_ffn_Sg"], a["L0_ffn_Su"], a["L0_ffn_Sd"]
    wsh = np.ascontiguousarray(np.stack([Sg.reshape(2, 128, 4, 512), Su.reshape(2, 128, 4, 512),
                                         Sd.reshape(2, 4, 128, 512).transpose(0, 2, 1, 3)], 2))
    wex = np.concatenate([a["L0_ffn_Wg"].reshape(64, 128, 512), a["L0_ffn_Wu"].reshape(64, 128, 512),
                          a["L0_ffn_Wd"]], 2)
    tok = np.ascontiguousarray((np.arange(128)[:, None] + 128 * np.arange(NT)[None]).astype(np.int32))
    arrays = {"x_in": np.ascontiguousarray(a["x"]), "ctx_in": ctxT, "par_in": par, "wsh_in": wsh, "wex_in": wex,
              "tok_in": tok}
    nc = _bacc.Bacc("TRN2", target_bir_lowering=False, num_devices=1)
    args = [nc.dram_tensor(n, v.shape, mybir.dt.from_np(v.dtype), kind="ExternalInput").ap()
            for n, v in arrays.items()]
    o = nc.dram_tensor("out_0", (B, T, D), mybir.dt.float32, kind="ExternalOutput").ap()
    build(nc, *args, o)
    r = _run(nc, [arrays], core_ids=[0])
    return r.results[0]["out_0"]
```

```python
import numpy as np
import concourse.bass as bass
from concourse import mybir
from contextlib import ExitStack

B, T, D, C, DK = 4, 512, 512, 256, 128
E, F, KTOP, ND, NSH = 64, 128, 4, 4, 2
NT = B * T // 128
NTILE = E + 63
PAR = {}


def _layout():
    at = 0
    for name, w in (("wq", 256), ("wk", 256), ("bqk", 2), ("g", 2), ("eps", 1), ("ident", 128), ("rb", 64), ("wr", 256),
                    ("te1", 1024), ("tb1", 2), ("te2", 8), ("tb2", 4), ("aff", 256), ("iota", 64),
                    ("iota128", 64), ("mean", 1), ("half", 128), ("tri", 128), ("one", 128)):
        PAR[name] = (at, at + w)
        at += w
    return at


PARW = _layout()
PAR1 = PAR["ident"][1]
PRE, EVERY, DYN = 6, 4, 32


class Queues:

    def __init__(self, nc, ctx):
        self.nc, self.ctx = nc, ctx
        self.lists = {e: [] for e in ("pe", "act", "dve", "pool", "sp")}
        self.sems, self.count = {}, {}

    def sem(self, name):
        if name not in self.sems:
            self.sems[name] = self.ctx.enter_context(self.nc.semaphore(name))
            self.count[name] = 0
        return self.sems[name]

    def add(self, engine, f, waits=(), sig=None, by=1):
        waits = [w for w in waits if w is not None]
        out = None
        sem = None
        if sig is not None:
            sem = self.sem(sig)
            self.count[sig] += by
            out = (sig, self.count[sig])
        self.lists[engine].append(("op", f, waits, sem, by))
        return out

    def dma(self, engine, f, waits, sig):
        return self.add(engine, f, waits, sig, 16)

    def begin_if(self, engines, i):
        for e in engines:
            self.lists[e].append(("if", i))

    def end_if(self, engines):
        for e in engines:
            self.lists[e].append(("endif",))

    def play(self, name, eng, cond):
        todo = self.lists[name]
        seen = {}

        def run(at, local):
            while at < len(todo):
                item = todo[at]
                if item[0] == "op":
                    _, f, waits, sem, by = item
                    for s, v in waits:
                        if max(seen.get(s, 0), local.get(s, 0)) < v:
                            eng.wait_ge(self.sems[s], v)
                            local[s] = v
                    ins = f(eng)
                    if sem is not None:
                        ins.then_inc(sem, by)
                    at += 1
                elif item[0] == "if":
                    with eng.If(cond(eng, item[1])):
                        at = run(at + 1, dict(local))
                else:
                    return at + 1
            return at

        run(0, seen)


class Ring:

    def __init__(self, bufs):
        self.bufs, self.free, self.n = bufs, [()] * len(bufs), 0

    def take(self):
        i = self.n % len(self.bufs)
        self.n += 1
        return i, self.bufs[i], self.free[i]

    def give(self, i, *readers):
        self.free[i] = readers


def build(nc, x, ctxT, par, wsh, wex, tok, out):
    fp32, i32 = mybir.dt.float32, mybir.dt.int32
    u32 = mybir.dt.uint32
    ALU, ACT, AX = mybir.AluOpType, mybir.ActivationFunctionType, mybir.AxisListType
    ctx = ExitStack()
    with ctx:
        q = Queues(nc, ctx)
        add, dma = q.add, q.dma

        def sb(name, shape, dt=fp32):
            return ctx.enter_context(nc.sbuf_tensor(name, shape, dt))

        NW, NG, NYS = 5, 3, 3
        P_ = sb("par_sb", [128, PARW])

        def p(name, a=0, b=None):
            lo, hi = PAR[name]
            return P_[:, lo + a:(hi if b is None else lo + b)]

        acc = sb("acc", [128, NT, D])
        xT = sb("xT", [128, B, 4, T])
        shw = sb("shw", [128, NSH, 3, 4, 512])
        wall = sb("wall", [128, NW * 1536])
        W = [wall[:, 1536 * i:1536 * i + 1536] for i in range(NW)]
        xgall = sb("xgall", [128, NG * D])
        xg = [xgall[:, D * i:D * i + D] for i in range(NG)]
        work = sb("work", [128, 10 * 1024 // 4 * 4])
        small = sb("small", [128, 96])
        tokid = sb("tokid", [128, NT], i32)
        table = sb("table", [128, 128], i32)
        eid = sb("eid", [1, 66], i32)

        def cut(t, a, shape):
            n = int(np.prod(shape))
            v = t[:, a:a + n]
            if len(shape) == 2:
                v = v.rearrange("p (a b) -> p a b", a=shape[0])
            return v

        cx = [cut(work, 0, [2, 512]), cut(xgall, 0, [2, 512])]
        qs = cut(work, 1024, [512])
        ks = cut(work, 1536, [512])
        Am = [cut(work, 2048, [4, 512]), cut(wall, 0, [4, 512])]
        xn = [cut(work, 4096, [4, 512]), cut(wall, 2048, [4, 512])]
        AT = cut(work, 6144, [4, 512])
        xnT = cut(work, 8192, [4, 512])
        hs = [cut(work, 6144 + 512 * n, [512]) for n in range(8)]
        ohk = cut(wall, 0, [NT, E])
        cmpv = cut(wall, 1024, [32, 64])[0:1]
        lg, lb, ex, tmp = (cut(wall, 4096 + 256 * n, [4, E]) for n in range(4))
        Msum = cut(wall, 5120, [NT, E])
        Run = cut(wall, 6144, [NT, E])
        cnt = cut(wall, 7168, [8, E])
        slotd = cut(work, 2048, [NT, E])
        ssil = [sb(f"ssil{i}", [128, 512]) for i in range(2)]
        xgT = [cut(work, 0 + 512 * i, [4, 128]) for i in range(2)]
        sg = [cut(work, 1024 + 128 * i, [128]) for i in range(2)]
        hh = [cut(work, 1280 + 128 * i, [128]) for i in range(2)]
        ysb = [cut(work, 1536 + 512 * i, [512]) for i in range(NYS)]
        yg = [cut(work, 3072 + 512 * i, [512]) for i in range(6)]

        bank = [ctx.enter_context(nc.psum_tensor(f"bank{i}", [128, 512], fp32)) for i in range(8)]

        xnd = nc.dram_tensor("xnd", (NT * 128, D), fp32)
        tabd = nc.dram_tensor("tabd", (128 * 128, 1), i32)
        yd = nc.dram_tensor("yd", (NTILE * 128, D), fp32)

        t_x, t_cx = {}, {}
        t_par = dma("act", lambda e: e.dma_start(P_[:, 0:PAR1], par[:, 0:PAR1]), (), "d_par")
        t_x, t_cx = {}, {}

        def load_x(b):
            t_x[b] = dma("sp", lambda e: e.dma_start(
                acc[:, 4 * b:4 * b + 4, :], x[b].rearrange("(c p) d -> p c d", p=128)), (), f"d_x{b}")

        def load_cx(b, waits):
            t_cx[b] = dma("sp", lambda e: e.dma_start(cx[b % 2], ctxT[b]), waits, f"d_cx{b % 2}")

        load_x(0)
        load_cx(0, ())
        load_cx(1, ())
        load_x(1)
        t_par2 = dma("sp", lambda e: e.dma_start(P_[:, PAR1:PARW], par[:, PAR1:PARW]), (), "d_par2")
        load_x(2)
        load_x(3)
        t_tok = dma("sp", lambda e: e.dma_start(tokid[:, :], tok), (), "d_tok")
        t_sh = [dma("sp", lambda e, i=i: e.dma_start(shw[:, i, :, :, :], wsh[i]), (), f"d_sh{i}") for i in range(NSH)]
        t_z = add("dve", lambda e: e.memset(table[:, :], 0), (), "zero")
        t_tab0 = dma("sp", lambda e: e.dma_start(
            tabd.ap().rearrange("(a b) o -> a (b o)", b=128), table[:, :]), [t_z], "d_tab0")
        t_zy = []

        def zero_overflow(waits):
            for n in range(4):
                t_zy.append(dma("sp", lambda e, n=n: e.dma_start(
                    yd.ap()[128 * E:, 128 * n:128 * n + 128].rearrange("(t p) d -> p t d", p=128),
                    table[:, :].bitcast(fp32).unsqueeze(1).to_broadcast([128, NTILE - E, 128])), waits, f"d_zy{n}"))

        t_tanh = add("act", lambda e: e.activation(small[:, 0:2], p("g"), ACT.Tanh), [t_par], "tanh")
        tg1, tg2 = small[:, 0:1], small[:, 1:2]

        banks = Ring(bank)

        def pe(f, waits=(), sig=None):
            return add("pe", f, waits, sig)

        def group(ms, waits, sig):
            t = None
            for n, (o, l, r, s0, s1) in enumerate(ms):
                t = pe(lambda e, o=o, l=l, r=r, s0=s0, s1=s1: e.matmul(o, l, r, start=s0, stop=s1),
                       waits if n == 0 else (), sig if n == len(ms) - 1 else None)
            return t

        def transposes(ms, waits, sig):
            t = None
            for n, (o, i) in enumerate(ms):
                t = pe(lambda e, o=o, i=i: e.transpose(o, i, p("ident")), waits if n == 0 else (),
                       sig if n == len(ms) - 1 else None)
            return t

        def evac(o, i, waits, sig):
            return add("act", lambda e: e.activation(o, i, ACT.Copy), waits, sig)

        stats = sb("stats", [128, 4, 6])
        mv = sb("mv", [128, 4, 2])
        rs = sb("rs", [128, 4])
        sd = sb("sd", [128, 4])
        mx = sb("mx", [128, 4])
        nmx = sb("nmx", [128, 4])
        sm = sb("sm", [128, 4])
        ri = sb("ri", [128, 4])

        def layernorm(b, ready):
            done = []
            for c in range(4):
                src = acc[:, 4 * b + c, :]
                t = add("dve", lambda e, c=c, src=src: e.bn_stats(stats[:, c, :], src), [ready[c]], "ln")
                t = add("dve", lambda e, c=c: e.bn_aggr(mv[:, c, :], stats[:, c, :]), [t], "ln")
            t = add("act", lambda e: e.activation(sd[:, :], mv[:, :, 1], ACT.Sqrt, bias=p("eps")), [t, t_par], "sd")
            t = add("dve", lambda e: e.reciprocal(rs[:, :], sd[:, :]), [t], "ln")
            for c in range(4):
                src = acc[:, 4 * b + c, :]
                done.append(add("dve", lambda e, c=c, src=src: e.tensor_scalar(
                    xn[b % 2][:, c, :], src, mv[:, c, 0:1], rs[:, c:c + 1], ALU.subtract, ALU.mult),
                    [t, *(st["xn_free", b % 2] if c == 0 else ())], "ln"))
            return done

        st = {"xnT_free": (), "qk_free": None, "xT": {}, "xnd": []}
        for n in range(2):
            st["xn_free", n] = st["at_free", n] = ()

        def scores(b):
            z = b % 2
            i0, pq, f0 = banks.take()
            tq = group([(pq[:, :], p("wq", 128 * c, 128 * c + 128), cx[z][:, c, :], c == 0, c == 1) for c in range(2)],
                       [t_par, t_cx[b], *f0], "qk")
            i1, pk, f1 = banks.take()
            tk = group([(pk[:, :], p("wk", 128 * c, 128 * c + 128), cx[z][:, c, :], c == 0, c == 1) for c in range(2)],
                       [*f1], "qk")
            st["cx_free", z] = tk
            if b + 2 < B:
                load_cx(b + 2, [tk])
            tq = add("act", lambda e: e.activation(qs, pq[:, :], ACT.Identity, bias=p("bqk", 0, 1)),
                     [tq, st["qk_free"]], "qs")
            tk = add("act", lambda e: e.activation(ks, pk[:, :], ACT.Identity, bias=p("bqk", 1, 2)),
                     [tk, st["qk_free"]], "ks")
            banks.give(i0, tq)
            banks.give(i1, tk)
            te = []
            for m in range(4):
                i, pb, f = banks.take()
                t = group([(pb[:, :], qs[:, 128 * m:128 * m + 128], ks, True, True)], [tq, tk, *f], "en")
                st["qk_free"] = t
                t1 = add("dve", lambda e, m=m, pb=pb: e.reduce_max(mx[:, m:m + 1], pb[:, :], AX.X), [t], "mx")
                t1 = add("dve", lambda e, m=m: e.tensor_scalar(nmx[:, m:m + 1], mx[:, m:m + 1], -1.0, None, ALU.mult),
                         [t1, st.get(("exp", m))], "mx")
                t2 = add("act", lambda e, m=m, pb=pb: e.activation(
                    Am[z][:, m, :], pb[:, :], ACT.Exp, bias=nmx[:, m:m + 1], accum_out=sm[:, m:m + 1]),
                    [t1, *(st["at_free", z] if m == 0 else ())], "exp")
                st[("exp", m)] = t2
                banks.give(i, t2)
                t3 = add("dve", lambda e, m=m: e.reciprocal(ri[:, m:m + 1], sm[:, m:m + 1]), [t2], "at")
                t3 = add("dve", lambda e, m=m: e.tensor_scalar(Am[z][:, m, :], Am[z][:, m, :], ri[:, m:m + 1], None,
                                                               ALU.mult), [t3], "at")
                te.append(t3)
            st["te", b] = te

        def norm1(b):
            st["ln", b] = layernorm(b, [t_x[b]] * 4)

        def turned(b):
            z = b % 2
            txT = []
            for n in range(4):
                i, pb, f = banks.take()
                t = transposes([(pb[:, 128 * c:128 * c + 128], xn[z][:, c, 128 * n:128 * n + 128]) for c in range(4)],
                               [*st["ln", b], *f], "tr")
                st["xn_free", z] = (t,)
                t = evac(xnT[:, n, :], pb[:, :], [t, *st["xnT_free"]], "xnT")
                banks.give(i, t)
                txT.append(t)
            tAT = []
            for n in range(4):
                i, pb, f = banks.take()
                t = transposes([(pb[:, 128 * m:128 * m + 128], Am[z][:, m, 128 * n:128 * n + 128]) for m in range(4)],
                               [*st["te", b], *f], "tr")
                st["at_free", z] = (t,)
                t = evac(AT[:, n, :], pb[:, :], [t, *st["xnT_free"]], "AT")
                banks.give(i, t)
                tAT.append(t)
            st["tT", b] = [*txT, *tAT]

        def mixed(b):
            tx = []
            for c in range(4):
                i, pb, f = banks.take()
                t = group([(pb[:, :], xnT[:, n, 128 * c:128 * c + 128], AT[:, n, :], n == 0, n == 3)
                           for n in range(4)], [*st["tT", b], *f], "xm")
                st["xnT_free"] = (t,)
                a = acc[:, 4 * b + c, :]
                t = add("dve", lambda e, a=a, pb=pb: e.scalar_tensor_tensor(a, pb[:, :], tg1, a, ALU.mult, ALU.add),
                        [t, t_tanh], "x1")
                banks.give(i, t)
                tx.append(t)
            st[("x1", b)] = tx

        def second_norm(b):
            z = b % 2
            ln = layernorm(b, st[("x1", b)])
            t = dma("sp", lambda e: e.dma_start(
                xnd.ap()[512 * b:512 * b + 512, :].rearrange("(c p) d -> p c d", p=128), xn[z]), ln, f"d_xn{b}")
            st["xnd"].append(t)
            st["store", b] = t
            st["ln2", b] = ln
            if b == 0:
                zero_overflow([t])

        def second_turn(b):
            z = b % 2
            ln, t = st["ln2", b], st["store", b]
            out_t = []
            for c in range(4):
                i, pb, f = banks.take()
                tp = transposes([(pb[:, 128 * k:128 * k + 128], xn[z][:, c, k:512:4]) for k in range(4)],
                                [*ln, *f], "tr")
                tt = evac(xT[:, b, :, 128 * c:128 * c + 128], pb[:, :].rearrange("p (k t) -> p k t", k=4), [tp], "xT")
                banks.give(i, tt)
                out_t.append(tt)
            i, pb, f = banks.take()
            tm = group([(pb[:, k:k + 1], xn[z][:, c, k:512:4], p("mean"), c == 0, c == 3)
                        for k in range(4) for c in range(4)], [t_par2, *f], "xm1")
            st["xn_free", z] = (tm, t)
            tm2 = add("dve", lambda e: e.tensor_copy(small[:, 4 + 4 * b:8 + 4 * b], pb[:, 0:4]), [tm], "xms")
            banks.give(i, tm2)
            st["xT"][b] = out_t
            st[("xm", b)] = tm2

        def task_hidden(b):
            i, pb, f = banks.take()
            te1 = p("te1").rearrange("p (k j) -> p k j", k=4)
            t = group([(pb[:, j:j + 1], te1[:, k, 128 * j:128 * j + 128], small[:, 4 + 4 * b + k:5 + 4 * b + k],
                        k == 0, k == 3) for j in range(2) for k in range(4)], [st[("xm", b)], *f], "h1")
            for j in range(2):
                t1 = add("act", lambda e, j=j: e.activation(small[:, 20 + 2 * b + j:21 + 2 * b + j], pb[:, j:j + 1],
                                                            ACT.Gelu, bias=p("tb1", j, j + 1)), [t], "gelu")
            banks.give(i, t1)
            st[("h1", b)] = t1

        row = sb("row", [1, 4, 80])

        def task_dist(b):
            i, pb, f = banks.take()
            te2 = p("te2").rearrange("p (j n) -> p j n", j=2)
            t = group([(pb[0:1, 0:4], small[:, 20 + 2 * b + j:21 + 2 * b + j], te2[:, j, :], j == 0, j == 1)
                       for j in range(2)], [st[("h1", b)], *f], "l2")
            r = row[:, b, :]
            t = add("dve", lambda e: e.tensor_tensor(r[:, 0:4], pb[0:1, 0:4], p("tb2")[0:1, :], ALU.add), [t], "td")
            banks.give(i, t)
            t = add("dve", lambda e: e.reduce_max(r[:, 8:9], r[:, 0:4], AX.X), [t], "td")
            t = add("dve", lambda e: e.tensor_scalar(r[:, 9:10], r[:, 8:9], -1.0, None, ALU.mult), [t], "td")
            t = add("act", lambda e: e.activation(r[:, 4:8], r[:, 0:4], ACT.Exp, bias=r[:, 9:10],
                                                  accum_out=r[:, 10:11]), [t], "tde")
            t = add("dve", lambda e: e.reciprocal(r[:, 11:12], r[:, 10:11]), [t], "td")
            t = add("dve", lambda e: e.tensor_scalar(r[:, 12:16], r[:, 4:8], r[:, 11:12], None, ALU.mult), [t], "td")
            d = r[:, 16:80]
            aff = p("aff").rearrange("p (n e) -> p n e", n=4)
            t = add("dve", lambda e: e.tensor_scalar(d, aff[0:1, 0, :], r[:, 12:13], None, ALU.mult), [t], "td")
            for n in range(1, 4):
                t = add("dve", lambda e, n=n: e.scalar_tensor_tensor(d, aff[0:1, n, :], r[:, 12 + n:13 + n], d,
                                                                     ALU.mult, ALU.add), [t], "td")
            st[("dom", b)] = t

        v8 = sb("v8", [128, 4, 8])
        i8 = sb("i8", [128, 4, 8], u32)
        i8f = sb("i8f", [128, NT, 8])
        rmx = sb("rmx", [128, 4])
        Zs = sb("Zs", [128, NT])
        Es = sb("Es", [128, 4, NT])

        def bc(ap, shape):
            return ap.to_broadcast(shape)

        def router(b):
            i, pb, f = banks.take()
            wr = p("wr").rearrange("p (k e) -> p k e", k=4)
            ms = []
            for c in range(4):
                o = pb[:, 64 * c:64 * c + 64]
                ms += [(o, xT[:, b, k, 128 * c:128 * c + 128], wr[:, k, :], k == 0, False) for k in range(4)]
                ms += [(o, p("half")[0:1, :], row[:, b, 16:80], False, True)]
            t = group(ms, [*st["xT"][b], st[("dom", b)], *f], "lg")
            t = add("dve", lambda e: e.tensor_copy(lg[:, :, :], pb[:, 0:256].rearrange("p (c e) -> p c e", c=4)),
                    [t, st.get("exr")], "rt")
            banks.give(i, t)
            t0 = add("dve", lambda e: e.tensor_tensor(lb[:, :, :], lg[:, :, :],
                                                     bc(p("rb").unsqueeze(1), [128, 4, E]), ALU.add), [t], "rt")
            t = add("dve", lambda e: e.tensor_reduce(rmx[:, :], lg[:, :, :], AX.X, ALU.max), [t], "rt")
            t = add("dve", lambda e: e.tensor_tensor(tmp[:, :, :], lg[:, :, :],
                                                     bc(rmx[:, :].unsqueeze(2), [128, 4, E]), ALU.subtract),
                    [t], "rt")
            tex = add("act", lambda e: e.activation(ex[:, :, :], tmp[:, :, :], ACT.Exp), [t], "rexp")
            for c in range(4):
                t = add("dve", lambda e, c=c: e.max(v8[:, c, :], lb[:, c, :]), [t0], "rt")
                t = add("dve", lambda e, c=c: e.max_index(i8[:, c, :], v8[:, c, :], lb[:, c, :]), [t], "rt")
            t = add("dve", lambda e: e.tensor_copy(i8f[:, 4 * b:4 * b + 4, :], i8[:, :, :]), [t], "rt")
            tz = add("dve", lambda e: e.tensor_reduce(Zs[:, 4 * b:4 * b + 4], ex[:, :, :], AX.X, ALU.add), [tex], "rt")
            M = Msum[:, 4 * b:4 * b + 4, :]
            for k in range(4):
                o = M if k == 0 else lg[:, :, :]
                to = add("dve", lambda e, k=k, o=o: e.tensor_tensor(
                    o, bc(p("iota").unsqueeze(1), [128, 4, E]), bc(i8f[:, 4 * b:4 * b + 4, k:k + 1], [128, 4, E]),
                    ALU.is_equal), [t], "rt")
                tt = add("dve", lambda e, o=o: e.tensor_tensor(tmp[:, :, :], o, ex[:, :, :], ALU.mult), [to], "rt")
                if k:
                    t = add("dve", lambda e: e.tensor_tensor(M, M, lg[:, :, :], ALU.add), [to], "rt")
                tt = add("dve", lambda e, k=k: e.tensor_reduce(Es[:, k, 4 * b:4 * b + 4], tmp[:, :, :], AX.X, ALU.add),
                         [tt], "rt")
            st[("M", b)] = t
            st["exr"] = tt
            for c in range(4):
                j = 4 * b + c
                if j == 0:
                    t = add("dve", lambda e: e.memset(Run[:, 0, :], 0.0), (), "rt")
                else:
                    t = add("dve", lambda e, j=j: e.tensor_tensor(Run[:, j, :], Run[:, j - 1, :], Msum[:, j - 1, :],
                                                                  ALU.add), [t], "rt")
            st[("R", b)] = t

        slot = cut(work, 0, [4, NT])
        sloti = sb("sloti", [128, 4, NT], i32)
        addr = sb("addr", [128, 4, NT], i32)
        ai = work[:, 64:128].bitcast(i32).rearrange("p (a b) -> p a b", a=4)
        cni = cnt[:, 6:8, :].bitcast(i32)
        wts = sb("wts", [128, 4, NT])
        wz = cut(work, 128, [4, NT])

        def dispatch():
            i2, pc, f2 = banks.take()
            tc = group([(pc[:, 0:64], p("one"), Run[:, NT - 1, :], True, False),
                        (pc[:, 0:64], p("one"), Msum[:, NT - 1, :], False, True)],
                       [st[("R", B - 1)], st[("M", B - 1)], *f2], "pos")
            ps = []
            for half in range(2):
                i, pb, f = banks.take()
                ms = []
                for j in range(8 * half, 8 * half + 8):
                    o = pb[:, 64 * (j % 8):64 * (j % 8) + 64]
                    ms += [(o, p("tri"), Msum[:, j, :], True, False), (o, p("one"), Run[:, j, :], False, True)]
                ps.append((i, pb, group(ms, [*f], "pos")))
            piece()
            st["pos"] = ps[1][2]
            t = add("dve", lambda e: e.tensor_scalar(cni[:, 0, :], pc[:, 0:64], -1.0, None, ALU.add), [tc], "dp")
            banks.give(i2, t)
            t = add("dve", lambda e: e.tensor_scalar(cni[:, 1, :], cni[:, 0, :], 7, None, ALU.arith_shift_right),
                    [t], "dp")
            t = add("dve", lambda e: e.tensor_scalar(cnt[:, 0, :], cni[:, 1, :], 0.0, None, ALU.max), [t], "dp")
            src, step = 0, 1
            while step < 64:
                dst = 1 if src != 1 else 2
                add("dve", lambda e, s=src, d=dst, n=step: e.tensor_copy(cnt[:, d, 0:n], cnt[:, s, 0:n]), [t], "dp")
                t = add("dve", lambda e, s=src, d=dst, n=step: e.tensor_tensor(
                    cnt[:, d, n:64], cnt[:, s, n:64], cnt[:, s, 0:64 - n], ALU.add), [t], "dp")
                src, step = dst, 2 * step
            incl = src
            t1 = add("dve", lambda e: e.tensor_tensor(cnt[:, 3, :], cnt[:, incl, :], cnt[:, 0, :], ALU.subtract),
                     [t], "dp")
            t1 = add("dve", lambda e: e.tensor_scalar(cnt[:, 4, :], cnt[:, 3, :], 63.0, 128.0, ALU.add, ALU.mult),
                     [t1], "dp")
            t1 = add("dve", lambda e: e.tensor_tensor(cnt[:, 5, :], cnt[:, 4, :], p("iota128"), ALU.subtract),
                     [t1], "dp")
            for half, (i, pb, tp) in enumerate(ps):
                v = pb[:, :].rearrange("p (j e) -> p j e", j=8)
                o = slotd[:, 8 * half:8 * half + 8, :]
                t2 = add("dve", lambda e, o=o, v=v: e.tensor_scalar(o, v, 128.0, None, ALU.is_ge), [tp, t1, *st["at_free", 0]],
                         "dp")
                t2 = add("dve", lambda e, o=o: e.tensor_tensor(o, o, bc(cnt[:, 5:6, :], [128, 8, E]), ALU.mult),
                         [t2], "dp")
                t2 = add("dve", lambda e, o=o, v=v: e.tensor_tensor(o, o, v, ALU.add), [t2], "dp")
                banks.give(i, t2)
                t2 = add("dve", lambda e, o=o: e.tensor_tensor(o, o, bc(p("iota128").unsqueeze(1), [128, 8, E]),
                                                               ALU.add), [t2], "dp")
            tsc = []
            piece()
            for k in range(4):
                t3 = add("dve", lambda e, k=k: e.tensor_tensor(
                    ohk, bc(p("iota").unsqueeze(1), [128, NT, E]), bc(i8f[:, :, k:k + 1], [128, NT, E]),
                    ALU.is_equal), [t2, *st["at_free", 1]] if k == 0 else [t3], "dp")
                t3 = add("dve", lambda e: e.tensor_tensor(ohk, ohk, slotd, ALU.mult), [t3], "dp")
                t3 = add("dve", lambda e, k=k: e.tensor_reduce(slot[:, k, :], ohk, AX.X, ALU.add),
                         [t3], "dp")
                t4 = add("dve", lambda e, k=k: e.tensor_copy(sloti[:, k, :], slot[:, k, :]), [t3], "dp")
                ta = add("dve", lambda e, k=k: e.tensor_scalar(ai[:, k, :], sloti[:, k, :], 127, 7, ALU.bitwise_and,
                                                               ALU.logical_shift_left), [t4], "dp")
                tb = add("dve", lambda e, k=k: e.tensor_scalar(addr[:, k, :], sloti[:, k, :], 7, None,
                                                               ALU.logical_shift_right), [t4], "dp")
                tb = add("dve", lambda e, k=k: e.tensor_tensor(addr[:, k, :], addr[:, k, :], ai[:, k, :],
                                                               ALU.bitwise_or), [ta, tb], "dp")
                for j in range(NT):
                    tsc.append(dma("pool", lambda e, j=j, k=k: e.indirect_dma_start(
                        tabd.ap()[:, :], bass.IndirectOffsetOnAxis(ap=addr[:, k, j:j + 1], axis=0),
                        tokid[:, j:j + 1], None), [tb, t_tab0, t_tok], "d_sc"))
                piece()
            st["slots"] = t4
            st["table"] = dma("pool", lambda e: e.dma_start(
                table[:, :], tabd.ap().rearrange("(a b) o -> a (b o)", b=128)), [tsc[-1]], "d_tab")
            for half in range(2):
                a = 32 * half
                t5 = add("dve", lambda e, a=a: e.tensor_tensor(
                    cmpv, bc(cnt[0:1, incl:incl + 1, :], [1, 32, 64]),
                    bc(p("iota", a, a + 32)[0:1, :].unsqueeze(2), [1, 32, 64]), ALU.is_le),
                    [t, *(st["xn_free", 1] if half == 0 else (t5,))], "dp")
                t5 = add("dve", lambda e, a=a: e.tensor_reduce(row[:, 0, a:a + 32], cmpv, AX.X, ALU.add), [t5], "dp")
            add("dve", lambda e: e.tensor_copy(eid[:, 64:65], cnt[0:1, incl, 63:64]), [t5], "dp")
            st["eid"] = add("dve", lambda e: e.tensor_scalar(eid[:, 0:64], row[:, 0, 0:64], 63.0, None, ALU.min),
                            [t5], "dp")
            piece()
            t6 = add("dve", lambda e: e.reciprocal(wz[:, 0, :], Zs[:, :]), [st["exr"]], "dw")
            for k in range(4):
                t6 = add("dve", lambda e, k=k: e.tensor_tensor(wts[:, k, :], Es[:, k, :], wz[:, 0, :], ALU.mult),
                         [t6], "dw")
            t6 = add("dve", lambda e: e.tensor_tensor(wz[:, 1, :], wts[:, 0, :], wts[:, 1, :], ALU.add), [t6], "dw")
            t6 = add("dve", lambda e: e.tensor_tensor(wz[:, 1, :], wz[:, 1, :], wts[:, 2, :], ALU.add), [t6], "dw")
            t6 = add("dve", lambda e: e.tensor_tensor(wz[:, 1, :], wz[:, 1, :], wts[:, 3, :], ALU.add), [t6], "dw")
            t6 = add("dve", lambda e: e.tensor_scalar(wz[:, 1, :], wz[:, 1, :], 1e-8, None, ALU.add), [t6], "dw")
            t6 = add("dve", lambda e: e.reciprocal(wz[:, 2, :], wz[:, 1, :]), [t6], "dw")
            t6 = add("dve", lambda e: e.tensor_scalar(wz[:, 2, :], wz[:, 2, :], tg2, None, ALU.mult),
                     [t6, t_tanh], "dw")
            for k in range(4):
                t6 = add("dve", lambda e, k=k: e.tensor_tensor(wts[:, k, :], wts[:, k, :], wz[:, 2, :], ALU.mult),
                         [t6], "dw")
            st["wts"] = t6

        shared = {"banks": banks, "free_h": {}, "h": {}, "sil": Ring(ssil), "n": 0}

        def up_piece(b, s, c):
            R = shared["banks"]
            i0, pg, f0 = R.take()
            i1, pu, f1 = R.take()
            hc = slice(128 * c, 128 * c + 128)
            w0 = [*st["xT"][b], t_sh[s]]
            tg_ = group([(pg[:, :], shw[:, s, 0, k, hc], xT[:, b, k, :], k == 0, k == 3) for k in range(4)],
                        [*w0, *f0], "sh")
            tu = group([(pu[:, :], shw[:, s, 1, k, hc], xT[:, b, k, :], k == 0, k == 3) for k in range(4)],
                       [*f1], "sh")
            si, sbuf, sf = shared["sil"].take()
            ts = add("act", lambda e: e.activation(sbuf[:, :], pg[:, :], ACT.Silu), [tg_, *sf], "silu")
            R.give(i0, ts)
            n = 4 * s + c
            th = add("dve", lambda e: e.tensor_tensor(hs[n], sbuf[:, :], pu[:, :], ALU.mult),
                     [ts, tu, *shared["free_h"].get(n, st["xnT_free"])], "hs")
            R.give(i1, th)
            shared["sil"].give(si, th)
            shared["h"][n] = th

        def down_piece(b, tc):
            R = shared["banks"]
            i, pb, f = R.take()
            t = group([(pb[:, :], hs[n][:, 128 * tc:128 * tc + 128], shw[:, n // 4, 2, n % 4, :], n == 0, n == 7)
                       for n in range(8)], [*shared["h"].values(), *f], "sh")
            if tc == 3:
                shared["free_h"] = {n: (t,) for n in range(8)}
            a = acc[:, 4 * b + tc, :]
            t = add("dve", lambda e: e.scalar_tensor_tensor(a, pb[:, :], tg2, a, ALU.mult, ALU.add),
                    [t, t_tanh, *st[("x1", b)]], "shacc")
            R.give(i, t)
            st[("shacc", 4 * b + tc)] = t

        pieces = []
        for b in range(B):
            pieces += [lambda b=b, s=s, c=c: up_piece(b, s, c) for s in range(NSH) for c in range(4)]
            pieces += [lambda b=b, tc=tc: down_piece(b, tc) for tc in range(4)]

        def piece(n=1):
            for _ in range(n):
                if pieces:
                    pieces.pop(0)()

        norm1(0)
        scores(0)
        turned(0)
        for b in range(B):
            if b + 1 < B:
                scores(b + 1)
            if b:
                second_turn(b - 1)
            if b + 1 < B:
                norm1(b + 1)
            if b > 1:
                router(b - 2)
            mixed(b)
            if b:
                task_hidden(b - 1)
            if b + 1 < B:
                turned(b + 1)
            second_norm(b)
            if b:
                task_dist(b - 1)
        router(2)
        piece()
        second_turn(3)
        task_hidden(3)
        piece()
        task_dist(3)
        router(3)
        piece()
        dispatch()
        piece(PRE)

        ENG = ("pe", "act", "dve", "pool", "sp")
        last = {}
        for i, r in enumerate(banks.free):
            last[i] = r
        sbanks = Ring([bank[0], bank[1]])
        sbanks.free = [last[0], last[1]]
        shared["banks"] = sbanks
        xtb = Ring([bank[2], bank[3]])
        gub = Ring([bank[4], bank[5]])
        yb = Ring([bank[6], bank[7]])
        for r, a in ((xtb, 2), (gub, 4), (yb, 6)):
            r.free = [last[a], last[a + 1]]
        stage_free = [*st["xn_free", 0], *st["xn_free", 1], st["slots"], st["eid"], st["wts"], t_cx[B - 1]]
        tT, tG, tY, tW, tX, tEx, tEy, tYd = {}, {}, {}, {}, {}, {}, {}, {}
        tS, tH = {}, {}

        def load_weights(t):
            w = W[t % NW]
            waits = [tY.get(t - NW), *((st["slots"], *stage_free) if t < NW else ())]
            if t < E:
                tW[t] = dma("sp", lambda e: e.dma_start(w, wex[t]), waits, f"d_w{t % NW}")
            else:
                def f(e):
                    r = e.value_load(eid[0:1, t - E:t - E + 1], min_val=0, max_val=E - 1)
                    return e.dma_start(w, wex[bass.ds(r, 1), :, :].rearrange("o p n -> (o p) n"))
                tW[t] = dma("sp", f, [*waits, st["eid"]], f"d_w{t % NW}")

        def gather(t):
            tX[t] = dma("pool", lambda e: e.indirect_dma_start(
                xg[t % NG][:, :], None, xnd.ap()[:, :], bass.IndirectOffsetOnAxis(ap=table[:, t:t + 1], axis=0)),
                [st["table"], *st["xnd"], tT.get(t - NG), *(stage_free if t < NG else ())], f"d_g{t % NG}")

        def turn_tile(t):
            i, pb, f = xtb.take()
            g = xg[t % NG]
            tT[t] = transposes([(pb[:, 128 * k:128 * k + 128], g[:, k:512:4]) for k in range(4)],
                               [tX[t], *f], "eT")
            o = xgT[t % 2]
            tEx[t] = add("act", lambda e: e.activation(o, pb[:, :].rearrange("p (k t) -> p k t", k=4), ACT.Copy),
                         [tT[t], tG.get(t - 2), *(stage_free if t < 2 else ())], "eX")
            xtb.give(i, tEx[t])

        def up_tile(t):
            i, pb, f = gub.take()
            w, xx = W[t % NW], xgT[t % 2]
            tG[t] = group([(pb[:, 128 * m:128 * m + 128], w[:, 512 * m + 128 * k:512 * m + 128 * k + 128], xx[:, k, :],
                            k == 0, k == 3) for m in range(2) for k in range(4)], [tW[t], tEx[t], *f], "eG")
            s, h = sg[t % 2], hh[t % 2]
            tS[t] = add("act", lambda e: e.activation(s, pb[:, 0:128], ACT.Silu), [tG[t], tH.get(t - 2), *(stage_free if t < 2 else ())], "eS")
            tH[t] = add("dve", lambda e: e.tensor_tensor(h, s, pb[:, 128:256], ALU.mult), [tS[t], tY.get(t - 2)],
                        "eH")
            gub.give(i, tH[t])

        def down_tile(t):
            i, pb, f = yb.take()
            w = W[t % NW]
            tY[t] = group([(pb[:, :], hh[t % 2], w[:, 1024:1536], True, True)], [tH[t], *f], "eY")
            o = ysb[t % NYS]
            tEy[t] = add("dve", lambda e: e.tensor_copy(o, pb[:, :]), [tY[t], tYd.get(t - NYS),
                                                                         *(stage_free if t < 2 else ())], "eE")
            yb.give(i, tEy[t])
            tYd[t] = dma("sp", lambda e: e.dma_start(yd.ap()[128 * t:128 * t + 128, :], o), [tEy[t], *(t_zy if t == E else ())],
                         f"d_y{t % NYS}")

        for t in range(NW - 1):
            load_weights(t)
        for t in range(NG):
            gather(t)
        turn_tile(0)
        conds = {}

        def cond(eng, i):
            if id(eng) not in conds:
                conds[id(eng)] = eng.value_load(eid[0:1, 64:65], min_val=0, max_val=63)
            n = conds[id(eng)]
            return n == i[1] if isinstance(i, tuple) else n > i - 1

        def iteration(i):
            if i + 1 < NTILE:
                turn_tile(i + 1)
            if i < NTILE:
                up_tile(i)
            if 1 <= i and i - 2 + NW < NTILE:
                load_weights(i - 2 + NW)
            if i + NG < NTILE:
                gather(i + NG)

        for i in range(NTILE + 1):
            dyn = i > E
            if dyn and (i - E) % EVERY == 1 and i < E + DYN:
                piece()
            if i == E:
                for e in ENG:
                    q.add(e, lambda eng: conds.setdefault(id(eng), eng.value_load(
                        eid[0:1, 64:65], min_val=0, max_val=63)), [st["eid"]])
            if dyn:
                q.begin_if(ENG, i - E)
            iteration(i)
            if not dyn and i % EVERY == 3:
                piece()
            if i >= 1:
                down_tile(i - 1)
            if i == E:
                q.add("sp", lambda e: None, [tYd[i - 3]])
            if i >= E:
                q.add("sp", lambda e: None, [tYd[i - 2]])
            if dyn:
                q.end_if(ENG)
            if i >= E:
                q.begin_if(("sp",), ("eq", i - E))
                q.add("sp", lambda e: None, [tYd[i - 1]])
                q.end_if(("sp",))

        t_all = add("sp", lambda e: e.nop(), (), "yall")
        ra = add("act", lambda e: e.activation(small[:, 80:81], small[:, 0:1], ACT.Copy), (), "endA")
        rv = add("dve", lambda e: e.tensor_copy(small[:, 81:82], small[:, 0:1]), (), "endV")
        fb = Ring(bank)
        fb.free = [*sbanks.free] + [(ra, rv)] * 6
        shared["banks"] = fb
        ygr = Ring(yg)
        tg_ = {}

        def fetch(j, k):
            i, g, f = ygr.take()
            t = dma("pool", lambda e: e.indirect_dma_start(
                g, None, yd.ap()[:, :], bass.IndirectOffsetOnAxis(ap=sloti[:, k, j:j + 1], axis=0)),
                [t_all, *f], f"d_yg{i}")
            tg_[(j, k)] = (i, g, t)

        def combine(j):
            for k in range(4):
                i, g, t = tg_[(j, k)]
                a = acc[:, j, :]
                t = add("dve", lambda e, a=a, g=g, k=k: e.scalar_tensor_tensor(a, g, wts[:, k, j:j + 1], a, ALU.mult,
                                                                                ALU.add),
                        [t, st["wts"], st[("shacc", j)] if k == 0 else last_c[0]], "comb")
                last_c[0] = t
                ygr.give(i, t)
            st[("comb", j)] = last_c[0]

        last_c = [None]
        NPOST = len(pieces) - 2
        outs = []

        def store(j):
            outs.append(dma("sp", lambda e: e.dma_start(out[j // 4, 128 * (j % 4):128 * (j % 4) + 128, :],
                                                        acc[:, j, :]), [st[("comb", j)]], "d_out"))

        piece(2)
        for j in range(NT):
            for k in range(4):
                fetch(j, k)
            combine(j)
            store(j)
            if j < 11:
                piece(round((j + 1) * NPOST / 11) - round(j * NPOST / 11))
        assert not pieces
        q.add("sp", lambda e: None, [outs[-1]])

        block = ctx.enter_context(nc.Block())

        @block.sync
        def _(e):
            q.play("sp", e, cond)

        @block.gpsimd
        def _(e):
            q.play("pool", e, cond)

        @block.scalar
        def _(e):
            q.play("act", e, cond)

        @block.vector
        def _(e):
            q.play("dve", e, cond)

        @block.tensor
        def _(e):
            q.play("pe", e, cond)


def kernel(**inputs):
    import concourse.bacc as _bacc
    from concourse.bass_utils import run_bass_kernel_spmd as _run

    a = {k: np.asarray(v) for k, v in inputs.items()}
    f = np.float32
    par = np.zeros((128, PARW), f)

    def put(name, v):
        lo, hi = PAR[name]
        par[:, lo:hi] = np.broadcast_to(v, (128, hi - lo))

    def rows(m, k):
        return m.reshape(k, 128, -1).transpose(1, 0, 2).reshape(128, -1)

    put("wq", rows(a["L0_xattn_Wq"].T, 2))
    put("wk", rows(a["L0_xattn_Wk"].T, 2))
    put("bqk", np.stack([a["L0_xattn_bq"], a["L0_xattn_bk"]], 1))
    put("g", np.array([a["g_xattn"][0], a["g_ffn"][0]])[None])
    put("ident", np.eye(128, dtype=f))
    put("rb", a["L0_ffn_router_bias"][None])
    put("wr", a["L0_ffn_Wr"].T.reshape(128, 256))
    put("te1", a["L0_ffn_te_W1"].T.reshape(128, 1024))
    put("tb1", a["L0_ffn_te_b1"].reshape(2, 128).T)
    put("te2", rows(a["L0_ffn_te_W2"].T, 2))
    put("tb2", a["L0_ffn_te_b2"][None])
    put("aff", a["L0_ffn_affinity"].T.reshape(1, 256))
    put("iota", np.arange(64, dtype=f)[None])
    put("iota128", 128 * np.arange(64, dtype=f)[None])
    put("mean", np.full((1, 1), 1 / 512, f))
    put("half", np.full((1, 128), 0.5, f))
    put("tri", np.triu(np.ones((128, 128), f), 1))
    put("one", np.ones((1, 128), f))
    put("eps", np.full((1, 1), 1e-5, f))
    ctxT = np.ascontiguousarray(a["ctx_1024"].transpose(0, 2, 1).reshape(4, 2, 128, 512).transpose(0, 2, 1, 3))
    Sg, Su, Sd = a["L0_ffn_Sg"], a["L0_ffn_Su"], a["L0_ffn_Sd"]
    wsh = np.ascontiguousarray(np.stack([Sg.reshape(2, 128, 4, 512), Su.reshape(2, 128, 4, 512),
                                         Sd.reshape(2, 4, 128, 512).transpose(0, 2, 1, 3)], 2))
    wex = np.concatenate([a["L0_ffn_Wg"].reshape(64, 128, 512), a["L0_ffn_Wu"].reshape(64, 128, 512),
                          a["L0_ffn_Wd"]], 2)
    tok = np.ascontiguousarray((np.arange(128)[:, None] + 128 * np.arange(NT)[None]).astype(np.int32))
    arrays = {"x_in": np.ascontiguousarray(a["x"]), "ctx_in": ctxT, "par_in": par, "wsh_in": wsh, "wex_in": wex,
              "tok_in": tok}
    nc = _bacc.Bacc("TRN2", target_bir_lowering=False, num_devices=1)
    args = [nc.dram_tensor(n, v.shape, mybir.dt.from_np(v.dtype), kind="ExternalInput").ap()
            for n, v in arrays.items()]
    o = nc.dram_tensor("out_0", (B, T, D), mybir.dt.float32, kind="ExternalOutput").ap()
    build(nc, *args, o)
    r = _run(nc, [arrays], core_ids=[0])
    return r.results[0]["out_0"]
```

```python
import numpy as np
import concourse.bass as bass
from concourse import mybir
from contextlib import ExitStack

B, T, D, C, DK = 4, 512, 512, 256, 128
E, F, KTOP, ND, NSH = 64, 128, 4, 4, 2
NT = B * T // 128
NTILE = E + 63
PAR = {}


def _layout():
    at = 0
    for name, w in (("wq", 256), ("wk", 256), ("bqk", 2), ("g", 2), ("ident", 128), ("rb", 64), ("wr", 256),
                    ("te1", 1024), ("tb1", 2), ("te2", 8), ("tb2", 4), ("aff", 256), ("iota", 64),
                    ("iota128", 64), ("half", 128), ("tri", 128), ("one", 128)):
        PAR[name] = (at, at + w)
        at += w
    return at


PARW = _layout()
PAR1 = PAR["ident"][1]
PRE, EVERY, DYN, STEP, POST = 3, 4, 32, 6, 16
UNITS = [(0, 0, 2, 2), (1, 0, 2, 1), (1, 1, 1, 1), (2, 2, 2, 1)]


class Queues:

    def __init__(self, nc, ctx):
        self.nc, self.ctx = nc, ctx
        self.lists = {e: [] for e in ("pe", "act", "dve", "pool", "sp")}
        self.sems, self.count = {}, {}

    def sem(self, name):
        if name not in self.sems:
            self.sems[name] = self.ctx.enter_context(self.nc.semaphore(name))
            self.count[name] = 0
        return self.sems[name]

    def add(self, engine, f, waits=(), sig=None, by=1):
        waits = [w for w in waits if w is not None]
        out = None
        sem = None
        if sig is not None:
            sem = self.sem(sig)
            self.count[sig] += by
            out = (sig, self.count[sig])
        self.lists[engine].append(("op", f, waits, sem, by))
        return out

    def dma(self, engine, f, waits, sig):
        return self.add(engine, f, waits, sig, 16)

    def begin_if(self, engines, i):
        for e in engines:
            self.lists[e].append(("if", i))

    def end_if(self, engines):
        for e in engines:
            self.lists[e].append(("endif",))

    def play(self, name, eng, cond):
        todo = self.lists[name]
        seen = {}

        def run(at, local):
            while at < len(todo):
                item = todo[at]
                if item[0] == "op":
                    _, f, waits, sem, by = item
                    for s, v in waits:
                        if max(seen.get(s, 0), local.get(s, 0)) < v:
                            eng.wait_ge(self.sems[s], v)
                            local[s] = v
                    ins = f(eng)
                    if sem is not None:
                        ins.then_inc(sem, by)
                    at += 1
                elif item[0] == "if":
                    with eng.If(cond(eng, item[1])):
                        at = run(at + 1, dict(local))
                else:
                    return at + 1
            return at

        run(0, seen)


class Ring:

    def __init__(self, bufs):
        self.bufs, self.free, self.n, self.held = bufs, [()] * len(bufs), 0, set()

    def take(self):
        while self.n % len(self.bufs) in self.held:
            self.n += 1
        i = self.n % len(self.bufs)
        self.n += 1
        self.held.add(i)
        return i, self.bufs[i], self.free[i]

    def give(self, i, *readers):
        self.held.remove(i)
        self.free[i] = readers


def build(nc, x, ctxT, par, wsh, wex, tok, out):
    fp32, i32 = mybir.dt.float32, mybir.dt.int32
    u32 = mybir.dt.uint32
    ALU, ACT, AX = mybir.AluOpType, mybir.ActivationFunctionType, mybir.AxisListType
    ctx = ExitStack()
    with ctx:
        q = Queues(nc, ctx)
        add, dma = q.add, q.dma

        def sb(name, shape, dt=fp32):
            return ctx.enter_context(nc.sbuf_tensor(name, shape, dt))

        NW, NG, NYS = 5, 3, 3
        P_ = sb("par_sb", [128, PARW])

        def p(name, a=0, b=None):
            lo, hi = PAR[name]
            return P_[:, lo + a:(hi if b is None else lo + b)]

        acc = sb("acc", [128, NT, D])
        xTm = sb("xTm", [128, B - 1, 4, T])
        hsm = sb("hsm", [128, 6, 512])
        shw = sb("shw", [128, NSH, 3, 4, 512])
        wall = sb("wall", [128, NW * 1536])
        W = [wall[:, 1536 * i:1536 * i + 1536] for i in range(NW)]
        xgall = sb("xgall", [128, NG * D])
        xg = [xgall[:, D * i:D * i + D] for i in range(NG)]
        work = sb("work", [128, 10240])
        small = sb("small", [128, 96])
        tokid = sb("tokid", [128, NT], i32)
        table = sb("table", [128, 128], i32)
        eid = sb("eid", [1, 66], i32)

        def cut(t, a, shape):
            n = int(np.prod(shape))
            v = t[:, a:a + n]
            if len(shape) == 2:
                v = v.rearrange("p (a b) -> p a b", a=shape[0])
            return v

        cx = [cut(work, 0, [2, 512]), cut(xgall, 0, [2, 512])]
        qs = cut(work, 1024, [512])
        ks = cut(work, 1536, [512])
        Am = [cut(work, 2048, [4, 512]), cut(wall, 0, [4, 512])]
        xn = [cut(work, 4096, [4, 512]), cut(wall, 2048, [4, 512])]
        AT = cut(work, 6144, [4, 512])
        xnT = cut(work, 8192, [4, 512])
        xT = [xTm[:, b, :, :] for b in range(B - 1)] + [xnT]
        hs0 = [hsm[:, n, :] for n in range(6)] + [cut(wall, 7168, [512]), cut(xgall, 1024, [512])]
        hs1 = [hsm[:, n, :] for n in range(6)] + [cut(work, 6144 + 512 * n, [512]) for n in range(2)]
        ohk = cut(wall, 0, [NT, E])
        cmpv = cut(wall, 1024, [32, 64])[0:1]
        lg, lb, ex, tmp = (cut(wall, 4096 + 256 * n, [4, E]) for n in range(4))
        Msum = wall[:, 5120:5632].bitcast(mybir.dt.bfloat16).rearrange("p (a b) -> p a b", a=NT)
        Run = wall[:, 6144:6656].bitcast(mybir.dt.bfloat16).rearrange("p (a b) -> p a b", a=NT)
        tri_one = wall[:, 5632:5760].bitcast(mybir.dt.bfloat16)
        tri, one = tri_one[:, 0:128], tri_one[:, 128:256]
        cnt = cut(xgall, 0, [8, E])
        slotd = cut(work, 2048, [NT, E])
        xgT = [cut(work, 0 + 512 * i, [4, 128]) for i in range(2)]
        sg = [cut(work, 1024 + 128 * i, [128]) for i in range(2)]
        hh = [cut(work, 1280 + 128 * i, [128]) for i in range(2)]
        ysb = [cut(work, 1536 + 512 * i, [512]) for i in range(NYS)]
        yg = [cut(work, a, [512]) for a in (*range(1536, 6144, 512), 7168, 7680)]

        bank = [ctx.enter_context(nc.psum_tensor(f"bank{i}", [128, 512], fp32)) for i in range(8)]

        xnd = nc.dram_tensor("xnd", (NT * 128, D), fp32)
        tabd = nc.dram_tensor("tabd", (128 * 128, 1), i32)
        yd = nc.dram_tensor("yd", (NTILE * 128, D), fp32)

        t_par = dma("act", lambda e: e.dma_start(P_[:, 0:PAR1], par[:, 0:PAR1]), (), "d_par")
        t_x, t_cx = {}, {}

        def load_x(b):
            t_x[b] = dma("sp", lambda e: e.dma_start(
                acc[:, 4 * b:4 * b + 4, :], x[b].rearrange("(c p) d -> p c d", p=128)), (), f"d_x{b}")

        def load_cx(b, waits):
            t_cx[b] = dma("sp", lambda e: e.dma_start(cx[b % 2], ctxT[b]), waits, f"d_cx{b % 2}")

        load_cx(0, ())
        load_x(0)
        load_cx(1, ())
        load_x(1)
        t_par2 = dma("sp", lambda e: e.dma_start(P_[:, PAR1:PARW], par[:, PAR1:PARW]), (), "d_par2")
        load_x(2)
        load_x(3)
        t_tok = dma("sp", lambda e: e.dma_start(tokid[:, :], tok), (), "d_tok")
        t_sh = [dma("sp", lambda e, i=i: e.dma_start(shw[:, i, :, :, :], wsh[i]), (), f"d_sh{i}") for i in range(NSH)]
        t_z = add("dve", lambda e: e.memset(table[:, :], 0), (), "zero")
        t_tab0 = dma("sp", lambda e: e.dma_start(
            tabd.ap().rearrange("(a b) o -> a (b o)", b=128), table[:, :]), [t_z], "d_tab0")
        t_zy = []

        def zero_overflow(waits):
            for n in range(4):
                t_zy.append(dma("sp", lambda e, n=n: e.dma_start(
                    yd.ap()[128 * E:, 128 * n:128 * n + 128].rearrange("(t p) d -> p t d", p=128),
                    table[:, :].bitcast(fp32).unsqueeze(1).to_broadcast([128, NTILE - E, 128])), [t_z, *waits], f"d_zy{n}"))

        t_tanh = add("act", lambda e: e.activation(small[:, 0:2], p("g"), ACT.Tanh), [t_par], "tanh")
        tg1, tg2 = small[:, 0:1], small[:, 1:2]

        banks = Ring(bank)

        def pe(f, waits=(), sig=None):
            return add("pe", f, waits, sig)

        def group(ms, waits, sig):
            t = None
            for n, (o, l, r, s0, s1) in enumerate(ms):
                t = pe(lambda e, o=o, l=l, r=r, s0=s0, s1=s1: e.matmul(o, l, r, start=s0, stop=s1),
                       waits if n == 0 else (), sig if n == len(ms) - 1 else None)
            return t

        def transposes(ms, waits, sig):
            t = None
            for n, (o, i) in enumerate(ms):
                t = pe(lambda e, o=o, i=i: e.transpose(o, i, p("ident")), waits if n == 0 else (),
                       sig if n == len(ms) - 1 else None)
            return t

        def evac(o, i, waits, sig):
            return add("act", lambda e: e.activation(o, i, ACT.Copy), waits, sig)

        stats = sb("stats", [128, 4, 6])
        mv = sb("mv", [128, 2, 4, 2])
        rs = sb("rs", [128, 2, 3, 4])
        mhalf = sb("mhalf", [128, 4])
        t_mh = add("pool", lambda e: e.memset(mhalf[:, :], -0.5), (), "mh")
        mx = sb("mx", [128, 4])
        nmx = sb("nmx", [128, 4])
        sm = sb("sm", [128, 4])
        ri = sb("ri", [128, 4])

        def layernorm(b, ready, split):
            done = []
            h = st["lns"] = 1 - st["lns"]
            m, sd, r, nb = mv[:, h], rs[:, h, 0, :], rs[:, h, 1, :], rs[:, h, 2, :]
            for c in range(4):
                src = acc[:, 4 * b + c, :]
                t = add("dve", lambda e, c=c, src=src: e.bn_stats(stats[:, c, :], src), [ready[c]], "ln")
                t = add("dve", lambda e, c=c: e.bn_aggr(m[:, c, :], stats[:, c, :]), [t, *st["ln_free", h]], "ln")
            tp = add("pool", lambda e: e.tensor_scalar(sd, m[:, :, 1], 1e-5, None, ALU.add), [t], "sd")
            t = tr = add("pool", lambda e: e.tensor_tensor(r, sd, mhalf[:, :], ALU.pow), [tp, t_mh], "sd")
            if split < 4:
                t = add("pool", lambda e: e.tensor_tensor(nb, m[:, :, 0], r, ALU.mult), [tr], "sd")
                t = add("pool", lambda e: e.tensor_scalar(nb, nb, -1.0, None, ALU.mult), [t], "sd")
            for c in range(4):
                src = acc[:, 4 * b + c, :]
                o = xn[b % 2][:, c, :]
                if c < split:
                    done.append(add("dve", lambda e, c=c, src=src, o=o: e.tensor_scalar(
                        o, src, m[:, c, 0:1], r[:, c:c + 1], ALU.subtract, ALU.mult),
                        [tr, *st["xn_free", b % 2]], "ln"))
                else:
                    done.append(add("act", lambda e, c=c, src=src, o=o: e.activation(
                        o, src, ACT.Identity, bias=nb[:, c:c + 1], scale=r[:, c:c + 1]),
                        [t, *st["xn_free", b % 2]], "lna"))
            st["ln_free", h] = done
            return done

        st = {"xnT_free": (), "qk_free": None, "xT": {}, "xnd": []}
        for n in range(2):
            st["xn_free", n] = st["at_free", n] = st["ln_free", n] = ()
        st["lns"] = 0

        def qk(b):
            z = b % 2
            i0, pq, f0 = banks.take()
            tq = group([(pq[:, :], p("wq", 128 * c, 128 * c + 128), cx[z][:, c, :], c == 0, c == 1) for c in range(2)],
                       [t_par, t_cx[b], *f0], "qk")
            i1, pk, f1 = banks.take()
            tk = group([(pk[:, :], p("wk", 128 * c, 128 * c + 128), cx[z][:, c, :], c == 0, c == 1) for c in range(2)],
                       [*f1], "qk")
            st["cx_free", z] = tk
            if b + 2 < B:
                load_cx(b + 2, [tk])
            tq = add("act", lambda e: e.activation(qs, pq[:, :], ACT.Identity, bias=p("bqk", 0, 1)),
                     [tq, st["qk_free"]], "qs")
            tk = add("act", lambda e: e.activation(ks, pk[:, :], ACT.Identity, bias=p("bqk", 1, 2)),
                     [tk, st["qk_free"]], "ks")
            banks.give(i0, tq)
            banks.give(i1, tk)
            st["qk", b] = tq, tk

        def energy(b):
            z = b % 2
            tq, tk = st["qk", b]
            te = []
            for m in range(4):
                i, pb, f = banks.take()
                t = group([(pb[:, :], qs[:, 128 * m:128 * m + 128], ks, True, True)], [tq, tk, *f], "en")
                st["qk_free"] = t
                t1 = add("dve", lambda e, m=m, pb=pb: e.reduce_max(mx[:, m:m + 1], pb[:, :], AX.X), [t], "mx")
                t1 = add("dve", lambda e, m=m: e.tensor_scalar(nmx[:, m:m + 1], mx[:, m:m + 1], -1.0, None, ALU.mult),
                         [t1, st.get(("exp", m))], "mx")
                t2 = add("act", lambda e, m=m, pb=pb: e.activation(
                    Am[z][:, m, :], pb[:, :], ACT.Exp, bias=nmx[:, m:m + 1], accum_out=sm[:, m:m + 1]),
                    [t1, *(st["at_free", z] if m == 0 else ())], "exp")
                st[("exp", m)] = t2
                banks.give(i, t2)
                t3 = add("dve", lambda e, m=m: e.reciprocal(ri[:, m:m + 1], sm[:, m:m + 1]), [t2, st.get(("ri", m))],
                         "at")
                if m % 2 == 0:
                    t3 = add("dve", lambda e, m=m: e.tensor_scalar(
                        Am[z][:, m, :], Am[z][:, m, :], ri[:, m:m + 1], None, ALU.mult), [t3], "at")
                else:
                    t3 = add("act", lambda e, m=m: e.activation(
                        Am[z][:, m, :], Am[z][:, m, :], ACT.Copy, scale=ri[:, m:m + 1]), [t3], "ata")
                    st["ri", m] = t3
                te.append(t3)
            st["te", b] = te

        def norm1(b):
            st["ln", b] = layernorm(b, [t_x[b]] * 4, 2 if b == 0 else 0)

        def turn_x(b):
            z = b % 2
            txT = []
            for n in range(4):
                i, pb, f = banks.take()
                t = transposes([(pb[:, 128 * c:128 * c + 128], xn[z][:, c, 128 * n:128 * n + 128]) for c in range(4)],
                               [*st["ln", b], *f], "tr")
                st["xn_free", z] = (t,)
                t = evac(xnT[:, n, :], pb[:, :], [t, *st["xnT_free"]], "xnT")
                banks.give(i, t)
                txT.append(t)
            st["tT", b] = txT

        def turn_A(b):
            z = b % 2
            tAT = []
            for n in range(4):
                i, pb, f = banks.take()
                t = transposes([(pb[:, 128 * m:128 * m + 128], Am[z][:, m, 128 * n:128 * n + 128]) for m in range(4)],
                               [*st["te", b], *f], "tr")
                st["at_free", z] = (t,)
                t = evac(AT[:, n, :], pb[:, :], [t, *st["xnT_free"]], "AT")
                banks.give(i, t)
                tAT.append(t)
            st["tT", b] = [*st["tT", b], *tAT]

        def mixed(b):
            tx = []
            for c in range(4):
                i, pb, f = banks.take()
                t = group([(pb[:, :], xnT[:, n, 128 * c:128 * c + 128], AT[:, n, :], n == 0, n == 3)
                           for n in range(4)], [*st["tT", b], *f], "xm")
                st["xnT_free"] = (t,)
                a = acc[:, 4 * b + c, :]
                t = add("dve", lambda e, a=a, pb=pb: e.scalar_tensor_tensor(a, pb[:, :], tg1, a, ALU.mult, ALU.add),
                        [t, t_tanh], "x1")
                banks.give(i, t)
                tx.append(t)
            st[("x1", b)] = tx

        def second_norm(b):
            z = b % 2
            ln = layernorm(b, st[("x1", b)], 2)
            t = dma("sp", lambda e: e.dma_start(
                xnd.ap()[512 * b:512 * b + 512, :].rearrange("(c p) d -> p c d", p=128), xn[z]), ln, f"d_xn{b}")
            st["xnd"].append(t)
            st["store", b] = t
            st["ln2", b] = ln
            if b == 0:
                zero_overflow([t])

        def second_turn(b):
            z = b % 2
            ln, t = st["ln2", b], st["store", b]
            out_t = []
            for c in range(4):
                i, pb, f = banks.take()
                tp = transposes([(pb[:, 128 * k:128 * k + 128], xn[z][:, c, k:512:4]) for k in range(4)],
                                [ln[c], *f], "tr")
                tt = evac(xT[b][:, :, 128 * c:128 * c + 128], pb[:, :].rearrange("p (k t) -> p k t", k=4), [tp, *(st["xnT_free"] if b == B - 1 else ())], "xT")
                banks.give(i, tt)
                out_t.append(tt)
            st["xn_free", z] = (tp, t)
            tm = add("dve", lambda e: e.tensor_reduce(small[:, 4 + 4 * b:8 + 4 * b], xT[b], AX.X, ALU.add),
                     out_t, "xms")
            tm2 = add("dve", lambda e: e.tensor_scalar(small[:, 4 + 4 * b:8 + 4 * b], small[:, 4 + 4 * b:8 + 4 * b],
                                                       1.0 / T, None, ALU.mult), [tm], "xms")
            st["xT"][b] = out_t
            st[("xm", b)] = tm2

        def task_hidden(b):
            i, pb, f = banks.take()
            te1 = p("te1").rearrange("p (k j) -> p k j", k=4)
            t = group([(pb[:, j:j + 1], te1[:, k, 128 * j:128 * j + 128], small[:, 4 + 4 * b + k:5 + 4 * b + k],
                        k == 0, k == 3) for j in range(2) for k in range(4)], [st[("xm", b)], t_par2, *f], "h1")
            for j in range(2):
                t1 = add("act", lambda e, j=j: e.activation(small[:, 20 + 2 * b + j:21 + 2 * b + j], pb[:, j:j + 1],
                                                            ACT.Gelu, bias=p("tb1", j, j + 1)), [t], "gelu")
            banks.give(i, t1)
            st[("h1", b)] = t1

        row = sb("row", [1, 4, 80])

        def task_dist(b):
            i, pb, f = banks.take()
            te2 = p("te2").rearrange("p (j n) -> p j n", j=2)
            t = group([(pb[0:1, 0:4], small[:, 20 + 2 * b + j:21 + 2 * b + j], te2[:, j, :], j == 0, j == 1)
                       for j in range(2)], [st[("h1", b)], *f], "l2")
            r = row[:, b, :]
            t = add("dve", lambda e: e.tensor_tensor(r[:, 0:4], pb[0:1, 0:4], p("tb2")[0:1, :], ALU.add), [t], "td")
            banks.give(i, t)
            t = add("dve", lambda e: e.reduce_max(r[:, 8:9], r[:, 0:4], AX.X), [t], "td")
            t = add("dve", lambda e: e.tensor_scalar(r[:, 9:10], r[:, 8:9], -1.0, None, ALU.mult), [t], "td")
            t = add("act", lambda e: e.activation(r[:, 4:8], r[:, 0:4], ACT.Exp, bias=r[:, 9:10],
                                                  accum_out=r[:, 10:11]), [t], "tde")
            t = add("dve", lambda e: e.reciprocal(r[:, 11:12], r[:, 10:11]), [t], "td")
            t = add("dve", lambda e: e.tensor_scalar(r[:, 12:16], r[:, 4:8], r[:, 11:12], None, ALU.mult), [t], "td")
            d = r[:, 16:80]
            aff = p("aff").rearrange("p (n e) -> p n e", n=4)
            t = add("dve", lambda e: e.tensor_scalar(d, aff[0:1, 0, :], r[:, 12:13], None, ALU.mult), [t], "td")
            for n in range(1, 4):
                t = add("dve", lambda e, n=n: e.scalar_tensor_tensor(d, aff[0:1, n, :], r[:, 12 + n:13 + n], d,
                                                                     ALU.mult, ALU.add), [t], "td")
            st[("dom", b)] = t

        v8 = sb("v8", [128, 4, 8])
        i8 = sb("i8", [128, 4, 8], u32)
        i8f = sb("i8f", [128, NT, 8])
        rmx = sb("rmx", [128, 4])
        Zs = sb("Zs", [128, NT])
        Es = sb("Es", [128, 4, NT])

        def bc(ap, shape):
            return ap.to_broadcast(shape)

        def router(b):
            i, pb, f = banks.take()
            w0 = PAR["wr"][0]
            ms = []
            for c in range(4):
                o = pb[:, 96 * c:96 * c + 96]
                ms += [(o, xT[b][:, k, 128 * c:128 * c + 128], P_[:, w0 + 64 * k:w0 + 64 * k + 96], k == 0, False)
                       for k in range(4)]
                ms += [(o[:, 0:64], p("half")[0:1, :], row[:, b, 16:80], False, True)]
            t = group(ms, [*st["xT"][b], st[("dom", b)], *f], "lg")
            t = add("dve", lambda e: e.tensor_copy(lg[:, :, :], pb[:, 0:384].rearrange("p (c e) -> p c e", c=4)[:, :, 0:64]),
                    [t, st.get("exr")], "rt")
            banks.give(i, t)
            t0 = add("dve", lambda e: e.tensor_tensor(lb[:, :, :], lg[:, :, :],
                                                     bc(p("rb").unsqueeze(1), [128, 4, E]), ALU.add), [t], "rt")
            t = add("dve", lambda e: e.tensor_reduce(rmx[:, :], lg[:, :, :], AX.X, ALU.max), [t], "rt")
            t = add("dve", lambda e: e.tensor_tensor(tmp[:, :, :], lg[:, :, :],
                                                     bc(rmx[:, :].unsqueeze(2), [128, 4, E]), ALU.subtract),
                    [t, st.get(("tex", b - 1))], "rt")
            ex = exs[b]
            tex = add("act", lambda e: e.activation(ex, tmp[:, :, :], ACT.Exp), [t], "rexp")
            for c in range(4):
                t = add("dve", lambda e, c=c: e.max(v8[:, c, :], lb[:, c, :]), [t0], "rt")
                t = add("dve", lambda e, c=c: e.max_index(i8[:, c, :], v8[:, c, :], lb[:, c, :]), [t], "rt")
            t = add("dve", lambda e: e.tensor_copy(i8f[:, 4 * b:4 * b + 4, :], i8[:, :, :]), [t], "rt")
            st["tex", b] = tex
            M = Msum[:, 4 * b:4 * b + 4, :]
            for k in range(4):
                o = M if k == 0 else lg
                t = add("dve", lambda e, k=k, o=o: e.tensor_tensor(
                    o, bc(p("iota").unsqueeze(1), [128, 4, E]), bc(i8f[:, 4 * b:4 * b + 4, k:k + 1], [128, 4, E]),
                    ALU.is_equal), [t], "rt")
                if k:
                    t = add("dve", lambda e: e.tensor_tensor(M, M, lg, ALU.add), [t], "rt")
            st[("M", b)] = t
            for c in range(4):
                j = 4 * b + c
                if j == 0:
                    t = add("pool", lambda e: e.memset(Run[:, 0, :], 0.0), [t], "rp")
                else:
                    t = add("pool", lambda e, j=j: e.tensor_tensor(Run[:, j, :], Run[:, j - 1, :], Msum[:, j - 1, :],
                                                                  ALU.add), [t, st.get(("R", b - 1))], "rp")
            st[("R", b)] = t

        def chosen(b):
            ex = exs[b]
            td = add("dve", lambda e: e.tensor_reduce(Zs[:, 4 * b:4 * b + 4], ex, AX.X, ALU.add),
                     [st["tex", b]], "rt")
            for k in range(4):
                t = add("dve", lambda e, k=k: e.tensor_tensor(
                    lg, bc(p("iota").unsqueeze(1), [128, 4, E]), bc(i8f[:, 4 * b:4 * b + 4, k:k + 1], [128, 4, E]),
                    ALU.is_equal), [td], "rt")
                t = add("dve", lambda e: e.tensor_tensor(tmp, lg, ex, ALU.mult), [t], "rt")
                td = add("dve", lambda e, k=k: e.tensor_reduce(Es[:, k, 4 * b:4 * b + 4], tmp, AX.X, ALU.add),
                         [t], "rt")
            st["exr"] = td

        exs = [ex, ex, ex, cut(work, 576, [4, E])]
        slot = cut(work, 0, [4, NT])
        sloti = sb("sloti", [128, 4, NT], i32)
        addr = sb("addr", [128, 4, NT], i32)
        ai = work[:, 64:128].bitcast(i32).rearrange("p (a b) -> p a b", a=4)
        cni = cnt[:, 6:8, :].bitcast(i32)
        wts = sb("wts", [128, 4, NT])
        wz = cut(work, 192, [4, NT])

        def dispatch():
            i2, pc, f2 = banks.take()
            tc = group([(pc[:, 0:64], one, Run[:, NT - 1, :], True, False),
                        (pc[:, 0:64], one, Msum[:, NT - 1, :], False, True)],
                       [st[("R", B - 1)], st[("M", B - 1)], st["tri"], *f2], "pos")
            ps = []
            for half in range(2):
                i, pb, f = banks.take()
                h = slice(8 * half, 8 * half + 8)
                ps.append((i, pb, group([(pb[:, :], tri, Msum[:, h, :], True, False),
                                         (pb[:, :], one, Run[:, h, :], False, True)], [*f], "pos")))
            piece()
            t = add("dve", lambda e: e.tensor_scalar(cni[:, 0, :], pc[:, 0:64], -1.0, None, ALU.add), [tc], "dp")
            banks.give(i2, t)
            t = add("dve", lambda e: e.tensor_scalar(cni[:, 1, :], cni[:, 0, :], 7, None, ALU.arith_shift_right),
                    [t], "dp")
            t = add("dve", lambda e: e.tensor_scalar(cnt[:, 0, :], cni[:, 1, :], 0.0, None, ALU.max), [t], "dp")
            src, step = 0, 1
            while step < 64:
                dst = 1 if src != 1 else 2
                add("dve", lambda e, s=src, d=dst, n=step: e.tensor_copy(cnt[:, d, 0:n], cnt[:, s, 0:n]), [t], "dp")
                t = add("dve", lambda e, s=src, d=dst, n=step: e.tensor_tensor(
                    cnt[:, d, n:64], cnt[:, s, n:64], cnt[:, s, 0:64 - n], ALU.add), [t], "dp")
                src, step = dst, 2 * step
            incl = src
            t1 = add("dve", lambda e: e.tensor_tensor(cnt[:, 3, :], cnt[:, incl, :], cnt[:, 0, :], ALU.subtract),
                     [t], "dp")
            t1 = add("dve", lambda e: e.tensor_scalar(cnt[:, 4, :], cnt[:, 3, :], 63.0, 128.0, ALU.add, ALU.mult),
                     [t1], "dp")
            t1 = add("dve", lambda e: e.tensor_tensor(cnt[:, 5, :], cnt[:, 4, :], p("iota128"), ALU.subtract),
                     [t1], "dp")
            for half, (i, pb, tp) in enumerate(ps):
                v = pb[:, :].rearrange("p (j e) -> p j e", j=8)
                o = slotd[:, 8 * half:8 * half + 8, :]
                t2 = add("dve", lambda e, o=o, v=v: e.tensor_scalar(o, v, 128.0, None, ALU.is_ge), [tp, t1, *st["at_free", 0]],
                         "dp")
                t2 = add("dve", lambda e, o=o: e.tensor_tensor(o, o, bc(cnt[:, 5:6, :], [128, 8, E]), ALU.mult),
                         [t2], "dp")
                t2 = add("dve", lambda e, o=o, v=v: e.tensor_tensor(o, o, v, ALU.add), [t2], "dp")
                banks.give(i, t2)
                t2 = add("dve", lambda e, o=o: e.tensor_tensor(o, o, bc(p("iota128").unsqueeze(1), [128, 8, E]),
                                                               ALU.add), [t2], "dp")
            tsc = []
            unit(2)
            for k in range(4):
                t3 = add("dve", lambda e, k=k: e.tensor_tensor(
                    ohk, bc(p("iota").unsqueeze(1), [128, NT, E]), bc(i8f[:, :, k:k + 1], [128, NT, E]),
                    ALU.is_equal), [t2, *st["at_free", 1]] if k == 0 else [t3], "dp")
                t3 = add("dve", lambda e: e.tensor_tensor(ohk, ohk, slotd, ALU.mult), [t3], "dp")
                t3 = add("dve", lambda e, k=k: e.tensor_reduce(slot[:, k, :], ohk, AX.X, ALU.add),
                         [t3], "dp")
                t4 = add("dve", lambda e, k=k: e.tensor_copy(sloti[:, k, :], slot[:, k, :]), [t3], "dp")
                ta = add("dve", lambda e, k=k: e.tensor_scalar(ai[:, k, :], sloti[:, k, :], 127, 7, ALU.bitwise_and,
                                                               ALU.logical_shift_left), [t4], "dp")
                tb = add("dve", lambda e, k=k: e.tensor_scalar(addr[:, k, :], sloti[:, k, :], 7, None,
                                                               ALU.logical_shift_right), [t4], "dp")
                tb = add("dve", lambda e, k=k: e.tensor_tensor(addr[:, k, :], addr[:, k, :], ai[:, k, :],
                                                               ALU.bitwise_or), [ta, tb], "dp")
                for j in range(NT):
                    tsc.append(dma("pool", lambda e, j=j, k=k: e.indirect_dma_start(
                        tabd.ap()[:, :], bass.IndirectOffsetOnAxis(ap=addr[:, k, j:j + 1], axis=0),
                        tokid[:, j:j + 1], None), [tb, t_tab0, t_tok], "d_sc"))
                unit(2)
            st["slots"] = t4
            st["table"] = dma("pool", lambda e: e.dma_start(
                table[:, :], tabd.ap().rearrange("(a b) o -> a (b o)", b=128)), [tsc[-1]], "d_tab")
            for half in range(2):
                a = 32 * half
                t5 = add("dve", lambda e, a=a: e.tensor_tensor(
                    cmpv, bc(cnt[0:1, incl:incl + 1, :], [1, 32, 64]),
                    bc(p("iota", a, a + 32)[0:1, :].unsqueeze(2), [1, 32, 64]), ALU.is_le),
                    [t, *(st["xn_free", 1] if half == 0 else (t5,))], "dp")
                t5 = add("dve", lambda e, a=a: e.tensor_reduce(row[:, 0, a:a + 32], cmpv, AX.X, ALU.add), [t5], "dp")
            add("dve", lambda e: e.tensor_copy(eid[:, 64:65], cnt[0:1, incl, 63:64]), [t5], "dp")
            st["eid"] = add("dve", lambda e: e.tensor_scalar(eid[:, 0:64], row[:, 0, 0:64], 63.0, None, ALU.min),
                            [t5], "dp")
            chosen(B - 1)
            unit(8)
            t6 = add("dve", lambda e: e.reciprocal(wz[:, 0, :], Zs[:, :]), [st["exr"], st["slots"]], "dw")
            for k in range(4):
                t6 = add("dve", lambda e, k=k: e.tensor_tensor(wts[:, k, :], Es[:, k, :], wz[:, 0, :], ALU.mult),
                         [t6], "dw")
            t6 = add("dve", lambda e: e.tensor_tensor(wz[:, 1, :], wts[:, 0, :], wts[:, 1, :], ALU.add), [t6], "dw")
            t6 = add("dve", lambda e: e.tensor_tensor(wz[:, 1, :], wz[:, 1, :], wts[:, 2, :], ALU.add), [t6], "dw")
            t6 = add("dve", lambda e: e.tensor_tensor(wz[:, 1, :], wz[:, 1, :], wts[:, 3, :], ALU.add), [t6], "dw")
            t6 = add("dve", lambda e: e.tensor_scalar(wz[:, 1, :], wz[:, 1, :], 1e-8, None, ALU.add), [t6], "dw")
            t6 = add("dve", lambda e: e.reciprocal(wz[:, 2, :], wz[:, 1, :]), [t6], "dw")
            t6 = add("dve", lambda e: e.tensor_scalar(wz[:, 2, :], wz[:, 2, :], tg2, None, ALU.mult),
                     [t6, t_tanh], "dw")
            for k in range(4):
                t6 = add("dve", lambda e, k=k: e.tensor_tensor(wts[:, k, :], wts[:, k, :], wz[:, 2, :], ALU.mult),
                         [t6], "dw")
            st["wts"] = t6

        accw, sums, outs = {}, [0] * NT, []

        def added(j):
            sums[j] += 1
            if sums[j] == 2:
                outs.append(dma("sp", lambda e: e.dma_start(out[j // 4, 128 * (j % 4):128 * (j % 4) + 128, :],
                                                            acc[:, j, :]), [accw[j]], "d_out"))

        shared = {"banks": banks, "free_h": (), "h": {}, "n": 0}

        half = {}

        def up_gate(b, s, c):
            R = shared["banks"]
            i0, pg, f0 = R.take()
            hc = slice(128 * c, 128 * c + 128)
            t = group([(pg[:, :], shw[:, s, 0, k, hc], xT[b][:, k, :], k == 0, k == 3) for k in range(4)],
                      [*st["xT"][b], t_sh[s], *f0], "sh")
            n = 4 * s + c
            hs = hs1 if b else hs0
            half["silu"] = ts = add("act", lambda e: e.activation(hs[n], pg[:, :], ACT.Silu),
                                    [t, *shared["free_h"], *(st["xnT_free"] if b and n > 5 else ())], "silu")
            R.give(i0, ts)

        def up_rest(b, s, c):
            R = shared["banks"]
            i1, pu, f1 = R.take()
            hc = slice(128 * c, 128 * c + 128)
            tu = group([(pu[:, :], shw[:, s, 1, k, hc], xT[b][:, k, :], k == 0, k == 3) for k in range(4)],
                       [*f1], "sh")
            n = 4 * s + c
            hs = hs1 if b else hs0
            th = add("dve", lambda e: e.tensor_tensor(hs[n], hs[n], pu[:, :], ALU.mult), [half["silu"], tu], "hs")
            R.give(i1, th)
            shared["h"][n] = th

        def down_first(b, tc):
            R = shared["banks"]
            half["down"] = i, pb, f = R.take()
            half["open"] = True
            hs = hs1 if b else hs0
            group([(pb[:, :], hs[n][:, 128 * tc:128 * tc + 128], shw[:, n // 4, 2, n % 4, :], n == 0, False)
                   for n in range(4)], [*shared["h"].values(), *f], None)

        def down_rest(b, tc):
            R = shared["banks"]
            i, pb, f = half["down"]
            half["open"] = False
            hs = hs1 if b else hs0
            t = group([(pb[:, :], hs[n][:, 128 * tc:128 * tc + 128], shw[:, n // 4, 2, n % 4, :], False, n == 7)
                       for n in range(4, 8)], (), "sh")
            if tc == 3:
                shared["free_h"] = (t,)
            a = acc[:, 4 * b + tc, :]
            t = add("dve", lambda e: e.scalar_tensor_tensor(a, pb[:, :], tg2, a, ALU.mult, ALU.add),
                    [t, t_tanh, accw.get(4 * b + tc, st[("x1", b)][tc])], "shacc")
            R.give(i, t)
            accw[4 * b + tc] = t
            added(4 * b + tc)

        pieces = []
        for b in range(B):
            for s in range(NSH):
                for c in range(4):
                    pieces += [lambda b=b, s=s, c=c: up_gate(b, s, c), lambda b=b, s=s, c=c: up_rest(b, s, c)]
            for tc in range(4):
                pieces += [lambda b=b, tc=tc: down_first(b, tc), lambda b=b, tc=tc: down_rest(b, tc)]

        def unit(n=1):
            for _ in range(n):
                if pieces:
                    pieces.pop(0)()

        def piece(n=1):
            unit(2 * n)

        def close():
            if half.get("open"):
                unit()

        qk(0)
        norm1(0)
        energy(0)
        turn_x(0)
        qk(1)
        turn_A(0)
        norm1(1)
        energy(1)
        st["tri"] = add("dve", lambda e: e.tensor_copy(tri_one, p("tri", 0, 256)), [t_par2], "tri")
        for b in range(B):
            if b:
                router(b - 1)
            mixed(b)
            if b + 1 < B:
                turn_x(b + 1)
                turn_A(b + 1)
            second_norm(b)
            if b:
                chosen(b - 1)
            if b + 2 < B:
                qk(b + 2)
            unit(UNITS[b][0])
            second_turn(b)
            if b + 2 < B:
                energy(b + 2)
            unit(UNITS[b][1])
            task_hidden(b)
            unit(UNITS[b][2])
            task_dist(b)
            if b + 2 < B:
                norm1(b + 2)
            unit(UNITS[b][3])
        router(3)
        unit(3)
        dispatch()
        piece(2 * PRE)

        close()
        ENG = ("pe", "act", "dve", "pool", "sp")
        last = {}
        for i, r in enumerate(banks.free):
            last[i] = r
        sbanks = Ring([bank[0], bank[1]])
        sbanks.free = [last[0], last[1]]
        shared["banks"] = sbanks
        xtb = Ring([bank[2], bank[3]])
        gub = Ring([bank[4], bank[5]])
        yb = Ring([bank[6], bank[7]])
        for r, a in ((xtb, 2), (gub, 4), (yb, 6)):
            r.free = [last[a], last[a + 1]]
        assert len(pieces) <= 72
        stage_free = [*shared["free_h"], st["table"], *st["xn_free", 0], *st["xn_free", 1], st["slots"], st["eid"], st["wts"], t_cx[B - 1]]
        tT, tG, tY, tW, tX, tEx, tEy, tYd = {}, {}, {}, {}, {}, {}, {}, {}
        tS, tH = {}, {}

        def load_weights(t):
            w = W[t % NW]
            waits = [tY.get(t - NW), *((st["slots"], *stage_free) if t < NW else ())]
            if t < E:
                tW[t] = dma("sp", lambda e: e.dma_start(w, wex[t]), waits, f"d_w{t % NW}")
            else:
                def f(e):
                    r = e.value_load(eid[0:1, t - E:t - E + 1], min_val=0, max_val=E - 1)
                    return e.dma_start(w, wex[bass.ds(r, 1), :, :].rearrange("o p n -> (o p) n"))
                tW[t] = dma("sp", f, [*waits, st["eid"]], f"d_w{t % NW}")

        def gather(t):
            tX[t] = dma("pool", lambda e: e.indirect_dma_start(
                xg[t % NG][:, :], None, xnd.ap()[:, :], bass.IndirectOffsetOnAxis(ap=table[:, t:t + 1], axis=0)),
                [st["table"], *st["xnd"], tT.get(t - NG), *(stage_free if t < NG else ())], f"d_g{t % NG}")

        def turn_tile(t):
            i, pb, f = xtb.take()
            g = xg[t % NG]
            tT[t] = transposes([(pb[:, 128 * k:128 * k + 128], g[:, k:512:4]) for k in range(4)],
                               [tX[t], *f], "eT")
            o = xgT[t % 2]
            tEx[t] = add("act", lambda e: e.activation(o, pb[:, :].rearrange("p (k t) -> p k t", k=4), ACT.Copy),
                         [tT[t], tG.get(t - 2), *(stage_free if t < 2 else ())], "eX")
            xtb.give(i, tEx[t])

        def up_tile(t):
            i, pb, f = gub.take()
            w, xx = W[t % NW], xgT[t % 2]
            tG[t] = group([(pb[:, 128 * m:128 * m + 128], w[:, 512 * m + 128 * k:512 * m + 128 * k + 128], xx[:, k, :],
                            k == 0, k == 3) for m in range(2) for k in range(4)], [tW[t], tEx[t], *f], "eG")
            s, h = sg[t % 2], hh[t % 2]
            tS[t] = add("act", lambda e: e.activation(s, pb[:, 0:128], ACT.Silu), [tG[t], tH.get(t - 2), *(stage_free if t < 2 else ())], "eS")
            tH[t] = add("dve", lambda e: e.tensor_tensor(h, s, pb[:, 128:256], ALU.mult), [tS[t], tY.get(t - 2)],
                        "eH")
            gub.give(i, tH[t])

        def down_tile(t):
            i, pb, f = yb.take()
            w = W[t % NW]
            tY[t] = group([(pb[:, :], hh[t % 2], w[:, 1024:1536], True, True)], [tH[t], *f], "eY")
            o = ysb[t % NYS]
            tEy[t] = add("dve", lambda e: e.tensor_copy(o, pb[:, :]), [tY[t], tYd.get(t - NYS),
                                                                         *(stage_free if t < 2 else ())], "eE")
            yb.give(i, tEy[t])
            tYd[t] = dma("sp", lambda e: e.dma_start(yd.ap()[128 * t:128 * t + 128, :], o), [tEy[t], *(t_zy if t == E else ())],
                         f"d_y{t % NYS}")

        for t in range(NW - 1):
            load_weights(t)
        for t in range(NG):
            gather(t)
        turn_tile(0)
        conds = {}

        def cond(eng, i):
            if id(eng) not in conds:
                conds[id(eng)] = eng.value_load(eid[0:1, 64:65], min_val=0, max_val=63)
            n = conds[id(eng)]
            return n == i[1] if isinstance(i, tuple) else n > i - 1

        def iteration(i):
            if i + 1 < NTILE:
                turn_tile(i + 1)
            if i < NTILE:
                up_tile(i)
            if 1 <= i and i - 2 + NW < NTILE:
                load_weights(i - 2 + NW)
            if i + NG < NTILE:
                gather(i + NG)

        for i in range(NTILE + 1):
            dyn = i > E
            if dyn and (i - E) % EVERY == 1 and i < E + DYN:
                unit()
            if i == E:
                for e in ENG:
                    q.add(e, lambda eng: conds.setdefault(id(eng), eng.value_load(
                        eid[0:1, 64:65], min_val=0, max_val=63)), [st["eid"]])
            if dyn and (i - E) % EVERY == 1:
                q.begin_if(ENG, i - E)
            if dyn:
                q.begin_if(ENG, i - E)
            iteration(i)
            if not dyn and i % STEP == STEP - 1:
                unit()
            if i >= 1:
                down_tile(i - 1)
            if i == E:
                q.add("sp", lambda e: None, [tYd[i - 3]])
            if i >= E:
                q.add("sp", lambda e: None, [tYd[i - 2]])
            if dyn:
                q.end_if(ENG)
            if i >= E:
                q.begin_if(("sp",), ("eq", i - E))
                q.add("sp", lambda e: None, [tYd[i - 1]])
                q.end_if(("sp",))
            if dyn and ((i - E) % EVERY == 0 or i == NTILE):
                q.end_if(ENG)

        close()

        t_all = add("sp", lambda e: e.nop(), (), "yall")
        ra = add("act", lambda e: e.activation(small[:, 80:81], small[:, 0:1], ACT.Copy), (), "endA")
        rv = add("dve", lambda e: e.tensor_copy(small[:, 81:82], small[:, 0:1]), (), "endV")
        fb = Ring(bank)
        fb.free = [*sbanks.free] + [(ra, rv)] * 6
        shared["banks"] = fb
        ygr = Ring(yg)
        tg_ = {}

        def fetch(j, k):
            i, g, f = ygr.take()
            t = dma("pool", lambda e: e.indirect_dma_start(
                g, None, yd.ap()[:, :], bass.IndirectOffsetOnAxis(ap=sloti[:, k, j:j + 1], axis=0)),
                [t_all, *f], f"d_yg{i}")
            tg_[(j, k)] = (i, g, t)

        def combine(j):
            for k in range(4):
                i, g, t = tg_[(j, k)]
                a = acc[:, j, :]
                t = add("dve", lambda e, a=a, g=g, k=k: e.scalar_tensor_tensor(a, g, wts[:, k, j:j + 1], a, ALU.mult,
                                                                                ALU.add),
                        [t, st["wts"], accw.get(j, st["x1", j // 4][j % 4])], "comb")
                accw[j] = t
                ygr.give(i, t)
            added(j)

        NPOST = len(pieces) - 6
        unit(6)
        for j in range(NT):
            for k in range(4):
                fetch(j, k)
            combine(j)
            if j < POST:
                unit(round((j + 1) * NPOST / POST) - round(j * NPOST / POST))
        assert not pieces
        q.add("sp", lambda e: None, [outs[-1]])

        block = ctx.enter_context(nc.Block())

        @block.sync
        def _(e):
            q.play("sp", e, cond)

        @block.gpsimd
        def _(e):
            q.play("pool", e, cond)

        @block.scalar
        def _(e):
            q.play("act", e, cond)

        @block.vector
        def _(e):
            q.play("dve", e, cond)

        @block.tensor
        def _(e):
            q.play("pe", e, cond)


def kernel(**inputs):
    import concourse.bacc as _bacc
    from concourse.bass_utils import run_bass_kernel_spmd as _run

    a = {k: np.asarray(v) for k, v in inputs.items()}
    f = np.float32
    par = np.zeros((128, PARW), f)

    def put(name, v):
        lo, hi = PAR[name]
        par[:, lo:hi] = np.broadcast_to(v, (128, hi - lo))

    def rows(m, k):
        return m.reshape(k, 128, -1).transpose(1, 0, 2).reshape(128, -1)

    put("wq", rows(a["L0_xattn_Wq"].T, 2))
    put("wk", rows(a["L0_xattn_Wk"].T, 2))
    put("bqk", np.stack([a["L0_xattn_bq"], a["L0_xattn_bk"]], 1))
    put("g", np.array([a["g_xattn"][0], a["g_ffn"][0]])[None])
    put("ident", np.eye(128, dtype=f))
    put("rb", a["L0_ffn_router_bias"][None])
    put("wr", a["L0_ffn_Wr"].T.reshape(128, 256))
    put("te1", a["L0_ffn_te_W1"].T.reshape(128, 1024))
    put("tb1", a["L0_ffn_te_b1"].reshape(2, 128).T)
    put("te2", rows(a["L0_ffn_te_W2"].T, 2))
    put("tb2", a["L0_ffn_te_b2"][None])
    put("aff", a["L0_ffn_affinity"].T.reshape(1, 256))
    put("iota", np.arange(64, dtype=f)[None])
    put("iota128", 128 * np.arange(64, dtype=f)[None])
    put("half", np.full((1, 128), 0.5, f))
    put("tri", np.triu(np.ones((128, 128), f), 1))
    put("one", np.ones((1, 128), f))
    ctxT = np.ascontiguousarray(a["ctx_1024"].transpose(0, 2, 1).reshape(4, 2, 128, 512).transpose(0, 2, 1, 3))
    Sg, Su, Sd = a["L0_ffn_Sg"], a["L0_ffn_Su"], a["L0_ffn_Sd"]
    wsh = np.ascontiguousarray(np.stack([Sg.reshape(2, 128, 4, 512), Su.reshape(2, 128, 4, 512),
                                         Sd.reshape(2, 4, 128, 512).transpose(0, 2, 1, 3)], 2))
    wex = np.concatenate([a["L0_ffn_Wg"].reshape(64, 128, 512), a["L0_ffn_Wu"].reshape(64, 128, 512),
                          a["L0_ffn_Wd"]], 2)
    tok = np.ascontiguousarray((np.arange(128)[:, None] + 128 * np.arange(NT)[None]).astype(np.int32))
    arrays = {"x_in": np.ascontiguousarray(a["x"]), "ctx_in": ctxT, "par_in": par, "wsh_in": wsh, "wex_in": wex,
              "tok_in": tok}
    nc = _bacc.Bacc("TRN2", target_bir_lowering=False, num_devices=1)
    args = [nc.dram_tensor(n, v.shape, mybir.dt.from_np(v.dtype), kind="ExternalInput").ap()
            for n, v in arrays.items()]
    o = nc.dram_tensor("out_0", (B, T, D), mybir.dt.float32, kind="ExternalOutput").ap()
    build(nc, *args, o)
    r = _run(nc, [arrays], core_ids=[0])
    return r.results[0]["out_0"]
```
